# Optimizing a Trainium2 kernel written in Bass

```python
import numpy as np
import jax
import jax.numpy as jnp

def _softmax(x, axis=-1):
    return jax.nn.softmax(x, axis=axis)

def _gelu(x):
    return jax.nn.gelu(x, approximate=True)

def _silu(x):
    return jax.nn.silu(x)

def _sigmoid(x):
    return jax.nn.sigmoid(x)

def _layernorm(x, axis=-1, eps=1e-05):
    m = jnp.mean(x, axis=axis, keepdims=True)
    v = jnp.var(x, axis=axis, keepdims=True)
    return (x - m) / jnp.sqrt(v + eps)

def _scatter_add(tgt, idx, src, axis=0):
    return tgt.at[idx].add(src)

def _segment_sum(src, seg, n):
    return jax.ops.segment_sum(src, seg, n)
kernel_name = 'mk_recurrent_d2_jaxref_r8_6c4351'

def setup_inputs(seed: int=0):
    np.random.seed(seed)
    _w = jnp.asarray

    def _L0_attn_setup():
        import jax, jax.numpy as jnp
        import numpy as np
        D_INNER, D_STATE, DT_RANK = (128, 16, 32)

        def _selective_scan(x, x_proj_w, dt_proj_w, dt_proj_b, A_log, Dp):
            A = -jnp.exp(A_log)
            dbc = jnp.einsum('bld,nd->bln', x, x_proj_w)
            delta, Bm, Cm = jnp.split(dbc, [DT_RANK, DT_RANK + D_STATE], axis=-1)
            delta = jax.nn.softplus(jnp.einsum('blr,dr->bld', delta, dt_proj_w) + dt_proj_b)
            deltaA = jnp.exp(delta[..., None] * A)
            BX = delta[..., None] * Bm[:, :, None, :] * x[..., None]

            def comb(e1, e2):
                a1, b1 = e1
                a2, b2 = e2
                return (a2 * a1, a2 * b1 + b2)
            _, hs = jax.lax.associative_scan(comb, (deltaA, BX), axis=1)
            y = jnp.einsum('blds,bls->bld', hs, Cm)
            return y + Dp * x
        key = jax.random.key(seed)
        ks = jax.random.split(key, 12)
        B, L = (4, 256)
        A_row = jnp.log(jnp.arange(1, D_STATE + 1, dtype=jnp.float32))
        A_log = jnp.tile(A_row[None, :], (D_INNER, 1))
        s = 0.02
        return {'x': jax.random.normal(ks[0], (B, L, D_INNER), jnp.float32), 'x_proj_w': jax.random.normal(ks[1], (DT_RANK + 2 * D_STATE, D_INNER), jnp.float32) * s, 'dt_proj_w': jax.random.normal(ks[2], (D_INNER, DT_RANK), jnp.float32) * DT_RANK ** (-0.5), 'dt_proj_b': jax.random.normal(ks[3], (D_INNER,), jnp.float32) * 0.1 - 4.0, 'A_log': A_log, 'D': jnp.ones((D_INNER,), jnp.float32), 'x_proj_b_w': jax.random.normal(ks[4], (DT_RANK + 2 * D_STATE, D_INNER), jnp.float32) * s, 'dt_proj_b_w': jax.random.normal(ks[5], (D_INNER, DT_RANK), jnp.float32) * DT_RANK ** (-0.5), 'dt_proj_b_b': jax.random.normal(ks[6], (D_INNER,), jnp.float32) * 0.1 - 4.0, 'A_b_log': A_log, 'D_b': jnp.ones((D_INNER,), jnp.float32)}
    _L0_attn_in = _L0_attn_setup()

    def _L0_ffn_setup():
        import jax, jax.numpy as jnp
        import numpy as np
        NUM_EXPERTS = 8
        TOP_K = 2
        key = jax.random.key(seed)
        ks = jax.random.split(key, 4)
        B, S, H, F = (4, 512, 128, 512)
        x = jax.random.normal(ks[0], (B, S, H), dtype=jnp.float32)
        router_w = jax.random.normal(ks[1], (H, NUM_EXPERTS), dtype=jnp.float32) * 0.02
        w1 = jax.random.normal(ks[2], (H, F), dtype=jnp.float32) * 0.02
        b1 = jnp.zeros((F,), dtype=jnp.float32)
        w2 = jax.random.normal(ks[3], (F, H), dtype=jnp.float32) * 0.02
        b2 = jnp.zeros((H,), dtype=jnp.float32)
        return {'x': x, 'router_w': router_w, 'w1': w1, 'b1': b1, 'w2': w2, 'b2': b2}
    _L0_ffn_in = _L0_ffn_setup()

    def _L1_attn_setup():
        import jax, jax.numpy as jnp
        import numpy as np
        D_MODEL = 128
        NHEAD = 16
        HEAD_DIM = D_MODEL // NHEAD
        ROTARY_DIM = HEAD_DIM
        D_INNER = 2 * D_MODEL
        HEADDIM = 64
        H_SSM = D_INNER // HEADDIM
        D_STATE = 128
        D_CONV = 4
        CHUNK = 32
        CONV_DIM = D_INNER + 2 * D_STATE
        D_IN_PROJ = 2 * D_INNER + 2 * D_STATE + H_SSM
        EPS = 1e-05

        def rmsnorm(x, w):
            var = jnp.mean(x * x, axis=-1, keepdims=True)
            return x * jax.lax.rsqrt(var + EPS) * w

        def apply_rope(q):
            T = q.shape[1]
            half = ROTARY_DIM // 2
            inv_freq = 1.0 / 10000.0 ** (jnp.arange(0, ROTARY_DIM, 2, dtype=jnp.float32) / ROTARY_DIM)
            freqs = jnp.arange(T, dtype=jnp.float32)[:, None] * inv_freq[None, :]
            cos = jnp.cos(freqs)[None, :, None, :]
            sin = jnp.sin(freqs)[None, :, None, :]
            q1 = q[..., :half]
            q2 = q[..., half:ROTARY_DIM]
            rest = q[..., ROTARY_DIM:]
            return jnp.concatenate([q1 * cos - q2 * sin, q2 * cos + q1 * sin, rest], axis=-1)

        def segsum(x):
            T = x.shape[-1]
            xc = jnp.cumsum(x, axis=-1)
            ss = xc[..., :, None] - xc[..., None, :]
            mask = jnp.tril(jnp.ones((T, T), dtype=bool))
            return jnp.where(mask, ss, -jnp.inf)

        def ssd(x, dt, A, Bm, Cm):
            b, l, h, p = x.shape
            n = Bm.shape[-1]
            c = l // CHUNK
            xdt = (x * dt[..., None]).reshape(b, c, CHUNK, h, p)
            Adt = (dt * A).reshape(b, c, CHUNK, h).transpose(0, 3, 1, 2)
            Br = Bm.reshape(b, c, CHUNK, n)
            Cr = Cm.reshape(b, c, CHUNK, n)
            Acs = jnp.cumsum(Adt, axis=-1)
            Lmat = jnp.exp(segsum(Adt))
            Y_diag = jnp.einsum('bcln,bcsn,bhcls,bcshp->bclhp', Cr, Br, Lmat, xdt)
            decay_states = jnp.exp(Acs[..., -1:] - Acs)
            states = jnp.einsum('bcln,bhcl,bclhp->bchpn', Br, decay_states, xdt)
            A_chunk = jnp.pad(Acs[..., -1], ((0, 0), (0, 0), (1, 0)))
            decay_chunk = jnp.exp(segsum(A_chunk))
            states = jnp.concatenate([jnp.zeros_like(states[:, :1]), states], axis=1)
            new_states = jnp.einsum('bhzc,bchpn->bzhpn', decay_chunk, states)
            states_prev = new_states[:, :-1]
            Y_off = jnp.einsum('bcln,bchpn,bhcl->bclhp', Cr, states_prev, jnp.exp(Acs))
            return (Y_diag + Y_off).reshape(b, l, h, p)
        key = jax.random.key(seed)
        ks = jax.random.split(key, 8)
        B, T = (2, 256)
        return {'x': jax.random.normal(ks[0], (B, T, D_MODEL), dtype=jnp.float32), 'W_in': jax.random.normal(ks[1], (3 * D_MODEL, D_MODEL), dtype=jnp.float32) * 0.02, 'W_zxbcdt': jax.random.normal(ks[2], (D_IN_PROJ, D_MODEL), dtype=jnp.float32) * 0.02, 'conv_w': jax.random.normal(ks[3], (CONV_DIM, D_CONV), dtype=jnp.float32) * 0.2, 'conv_b': jnp.zeros((CONV_DIM,), dtype=jnp.float32), 'dt_bias': jax.random.normal(ks[4], (H_SSM,), dtype=jnp.float32) * 0.5, 'A_log': jax.random.normal(ks[5], (H_SSM,), dtype=jnp.float32) * 0.5, 'D_param': jax.random.normal(ks[6], (H_SSM,), dtype=jnp.float32), 'norm_pre_w': jnp.ones((D_MODEL,), dtype=jnp.float32), 'norm_gated_w': jnp.ones((D_INNER,), dtype=jnp.float32), 'W_out': jax.random.normal(ks[7], (D_MODEL, D_INNER), dtype=jnp.float32) * 0.02}
    _L1_attn_in = _L1_attn_setup()

    def _L1_ffn_setup():
        import jax, jax.numpy as jnp
        import numpy as np
        DIM = 128
        DEPTH = 2
        HEADS = 8
        DIM_HEAD = 64
        WINDOW = 64
        INNER = HEADS * DIM_HEAD
        HID = int(DIM * 4 * 2 / 3)
        B, N = (2, 1024)
        QK_SCALE = 8.0

        def shift_token(t):
            t1, t2 = jnp.split(t, 2, axis=-1)
            t2 = jnp.pad(t2, ((0, 0), (1, 0), (0, 0)))[:, :-1]
            return jnp.concatenate([t1, t2], axis=-1)

        def l2norm(t):
            return t / jnp.clip(jnp.linalg.norm(t, axis=-1, keepdims=True), 1e-12)

        def rotate_half(x):
            x1, x2 = jnp.split(x, 2, axis=-1)
            return jnp.concatenate([-x2, x1], axis=-1)

        def rotary_xpos(q, k):
            n = q.shape[-2]
            half_idx = jnp.arange(0, DIM_HEAD, 2, dtype=jnp.float32)
            inv_freq = 1.0 / 10000.0 ** (half_idx / DIM_HEAD)
            t = jnp.arange(n, dtype=jnp.float32)
            freqs = t[:, None] * inv_freq[None, :]
            freqs = jnp.concatenate([freqs, freqs], axis=-1)
            base = (half_idx + 0.4 * DIM_HEAD) / (1.4 * DIM_HEAD)
            power = (t - n // 2) / float(WINDOW // 2)
            scale = base[None, :] ** power[:, None]
            scale = jnp.concatenate([scale, scale], axis=-1)
            cos, sin = (jnp.cos(freqs), jnp.sin(freqs))
            q = q * cos * scale + rotate_half(q) * sin * scale
            k = k * cos / scale + rotate_half(k) * sin / scale
            return (q, k)

        def local_attention(q, k, v):
            b, h, n, d = q.shape
            w = n // WINDOW
            bq = q.reshape(b, h, w, WINDOW, d) * QK_SCALE
            bk = k.reshape(b, h, w, WINDOW, d)
            bv = v.reshape(b, h, w, WINDOW, d)

            def look_around(t):
                p = jnp.pad(t, ((0, 0), (0, 0), (1, 0), (0, 0), (0, 0)))
                return jnp.concatenate([p[:, :, :w], p[:, :, 1:]], axis=3)
            bk, bv = (look_around(bk), look_around(bv))
            bt = jnp.arange(n).reshape(w, WINDOW)
            btp = jnp.pad(bt, ((1, 0), (0, 0)), constant_values=-1)
            btk = jnp.concatenate([btp[:w], btp[1:]], axis=1)
            sim = jnp.einsum('bhwid,bhwjd->bhwij', bq, bk)
            i = bt[:, :, None]
            j = btk[:, None, :]
            mask = (i < j) | (i > j + WINDOW) | (j == -1)
            sim = jnp.where(mask, -jnp.finfo(sim.dtype).max, sim)
            attn = jax.nn.softmax(sim, axis=-1)
            out = jnp.einsum('bhwij,bhwjd->bhwid', attn, bv)
            return out.reshape(b, h, n, d)

        def _layer(x, wqkv, qs, ksc, wo, lg, lb, w1, b1, w2, b2):
            b, n, _ = x.shape
            h = shift_token(x)
            qkv = h @ wqkv
            q, k, v = jnp.split(qkv, 3, axis=-1)
            to_heads = lambda t: t.reshape(b, n, HEADS, DIM_HEAD).transpose(0, 2, 1, 3)
            q, k, v = (to_heads(q), to_heads(k), to_heads(v))
            q = l2norm(q) * qs
            k = l2norm(k) * ksc
            q, k = rotary_xpos(q, k)
            o = local_attention(q, k, v)
            o = o.transpose(0, 2, 1, 3).reshape(b, n, INNER)
            x = x + o @ wo
            h = shift_token(x)
            mu = h.mean(-1, keepdims=True)
            var = h.var(-1, keepdims=True)
            h = (h - mu) / jnp.sqrt(var + 1e-05) * lg + lb
            h = h @ w1 + b1
            a, g = jnp.split(h, 2, axis=-1)
            h = a * jax.nn.gelu(g, approximate=False)
            x = x + h @ w2 + b2
            return x
        key = jax.random.key(seed)
        ks = jax.random.split(key, 6)
        return {'x': jax.random.normal(ks[0], (B, N, DIM), jnp.float32), 'wqkv': jax.random.normal(ks[1], (DEPTH, DIM, 3 * INNER), jnp.float32) * 0.02, 'q_scale': jnp.ones((DEPTH, DIM_HEAD), jnp.float32), 'k_scale': jnp.ones((DEPTH, DIM_HEAD), jnp.float32), 'wo': jax.random.normal(ks[2], (DEPTH, INNER, DIM), jnp.float32) * 0.02, 'ln_g': jnp.ones((DEPTH, DIM), jnp.float32), 'ln_b': jnp.zeros((DEPTH, DIM), jnp.float32), 'w1': jax.random.normal(ks[3], (DEPTH, DIM, 2 * HID), jnp.float32) * 0.02, 'b1': jnp.zeros((DEPTH, 2 * HID), jnp.float32), 'w2': jax.random.normal(ks[4], (DEPTH, HID, DIM), jnp.float32) * 0.02, 'b2': jnp.zeros((DEPTH, DIM), jnp.float32)}
    _L1_ffn_in = _L1_ffn_setup()
    _d = {'L0_attn_x': _L0_attn_in['x'], 'L0_attn_x_proj_w': _L0_attn_in['x_proj_w'], 'L0_attn_dt_proj_w': _L0_attn_in['dt_proj_w'], 'L0_attn_dt_proj_b': _L0_attn_in['dt_proj_b'], 'L0_attn_A_log': _L0_attn_in['A_log'], 'L0_attn_D': _L0_attn_in['D'], 'L0_attn_x_proj_b_w': _L0_attn_in['x_proj_b_w'], 'L0_attn_dt_proj_b_w': _L0_attn_in['dt_proj_b_w'], 'L0_attn_dt_proj_b_b': _L0_attn_in['dt_proj_b_b'], 'L0_attn_A_b_log': _L0_attn_in['A_b_log'], 'L0_attn_D_b': _L0_attn_in['D_b'], 'L0_ffn_router_w': _L0_ffn_in['router_w'], 'L0_ffn_w1': _L0_ffn_in['w1'], 'L0_ffn_b1': _L0_ffn_in['b1'], 'L0_ffn_w2': _L0_ffn_in['w2'], 'L0_ffn_b2': _L0_ffn_in['b2'], 'L1_attn_W_in': _L1_attn_in['W_in'], 'L1_attn_W_zxbcdt': _L1_attn_in['W_zxbcdt'], 'L1_attn_conv_w': _L1_attn_in['conv_w'], 'L1_attn_conv_b': _L1_attn_in['conv_b'], 'L1_attn_dt_bias': _L1_attn_in['dt_bias'], 'L1_attn_A_log': _L1_attn_in['A_log'], 'L1_attn_D_param': _L1_attn_in['D_param'], 'L1_attn_norm_pre_w': _L1_attn_in['norm_pre_w'], 'L1_attn_norm_gated_w': _L1_attn_in['norm_gated_w'], 'L1_attn_W_out': _L1_attn_in['W_out'], 'L1_ffn_wqkv': _L1_ffn_in['wqkv'], 'L1_ffn_q_scale': _L1_ffn_in['q_scale'], 'L1_ffn_k_scale': _L1_ffn_in['k_scale'], 'L1_ffn_wo': _L1_ffn_in['wo'], 'L1_ffn_ln_g': _L1_ffn_in['ln_g'], 'L1_ffn_ln_b': _L1_ffn_in['ln_b'], 'L1_ffn_w1': _L1_ffn_in['w1'], 'L1_ffn_b1': _L1_ffn_in['b1'], 'L1_ffn_w2': _L1_ffn_in['w2'], 'L1_ffn_b2': _L1_ffn_in['b2']}
    _x0 = _d['L0_attn_x']
    _d['L0_attn_x'] = jax.random.normal(jax.random.fold_in(jax.random.key(seed), 1), (16, 512, 128), dtype=_x0.dtype)
    del _x0
    return _d

def reference(L0_attn_x, L0_attn_x_proj_w, L0_attn_dt_proj_w, L0_attn_dt_proj_b, L0_attn_A_log, L0_attn_D, L0_attn_x_proj_b_w, L0_attn_dt_proj_b_w, L0_attn_dt_proj_b_b, L0_attn_A_b_log, L0_attn_D_b, L0_ffn_router_w, L0_ffn_w1, L0_ffn_b1, L0_ffn_w2, L0_ffn_b2, L1_attn_W_in, L1_attn_W_zxbcdt, L1_attn_conv_w, L1_attn_conv_b, L1_attn_dt_bias, L1_attn_A_log, L1_attn_D_param, L1_attn_norm_pre_w, L1_attn_norm_gated_w, L1_attn_W_out, L1_ffn_wqkv, L1_ffn_q_scale, L1_ffn_k_scale, L1_ffn_wo, L1_ffn_ln_g, L1_ffn_ln_b, L1_ffn_w1, L1_ffn_b1, L1_ffn_w2, L1_ffn_b2):

    def _L0_attn_ref(x, x_proj_w, dt_proj_w, dt_proj_b, A_log, D, x_proj_b_w, dt_proj_b_w, dt_proj_b_b, A_b_log, D_b):
        import jax, jax.numpy as jnp
        import numpy as np
        D_INNER, D_STATE, DT_RANK = (128, 16, 32)

        def _selective_scan(x, x_proj_w, dt_proj_w, dt_proj_b, A_log, Dp):
            A = -jnp.exp(A_log)
            dbc = jnp.einsum('bld,nd->bln', x, x_proj_w)
            delta, Bm, Cm = jnp.split(dbc, [DT_RANK, DT_RANK + D_STATE], axis=-1)
            delta = jax.nn.softplus(jnp.einsum('blr,dr->bld', delta, dt_proj_w) + dt_proj_b)
            deltaA = jnp.exp(delta[..., None] * A)
            BX = delta[..., None] * Bm[:, :, None, :] * x[..., None]

            def comb(e1, e2):
                a1, b1 = e1
                a2, b2 = e2
                return (a2 * a1, a2 * b1 + b2)
            _, hs = jax.lax.associative_scan(comb, (deltaA, BX), axis=1)
            y = jnp.einsum('blds,bls->bld', hs, Cm)
            return y + Dp * x
        y = _selective_scan(x, x_proj_w, dt_proj_w, dt_proj_b, A_log, D)
        xb = x[:, ::-1]
        yb = _selective_scan(xb, x_proj_b_w, dt_proj_b_w, dt_proj_b_b, A_b_log, D_b)
        return y + yb[:, ::-1]

    def _L0_ffn_ref(x, router_w, w1, b1, w2, b2):
        import jax, jax.numpy as jnp
        import numpy as np
        NUM_EXPERTS = 8
        TOP_K = 2
        B, S, H = x.shape
        xt = x.reshape(-1, H)
        router_logits = jnp.matmul(xt, router_w)
        router_probs = jax.nn.softmax(router_logits, axis=-1)
        top_k_probs, top_k_indices = jax.lax.top_k(router_probs, TOP_K)
        top_k_probs = top_k_probs / jnp.sum(top_k_probs, axis=-1, keepdims=True)
        one_hot = jax.nn.one_hot(top_k_indices, NUM_EXPERTS, dtype=xt.dtype)
        combine = jnp.einsum('tk,tke->te', top_k_probs, one_hot)
        expert_out = jnp.matmul(jax.nn.gelu(jnp.matmul(xt, w1) + b1), w2) + b2
        out = expert_out * jnp.sum(combine, axis=-1, keepdims=True)
        return out.reshape(B, S, H)

    def _L1_attn_ref(x, W_in, W_zxbcdt, conv_w, conv_b, dt_bias, A_log, D_param, norm_pre_w, norm_gated_w, W_out):
        import jax, jax.numpy as jnp
        import numpy as np
        D_MODEL = 128
        NHEAD = 16
        HEAD_DIM = D_MODEL // NHEAD
        ROTARY_DIM = HEAD_DIM
        D_INNER = 2 * D_MODEL
        HEADDIM = 64
        H_SSM = D_INNER // HEADDIM
        D_STATE = 128
        D_CONV = 4
        CHUNK = 32
        CONV_DIM = D_INNER + 2 * D_STATE
        D_IN_PROJ = 2 * D_INNER + 2 * D_STATE + H_SSM
        EPS = 1e-05

        def rmsnorm(x, w):
            var = jnp.mean(x * x, axis=-1, keepdims=True)
            return x * jax.lax.rsqrt(var + EPS) * w

        def apply_rope(q):
            T = q.shape[1]
            half = ROTARY_DIM // 2
            inv_freq = 1.0 / 10000.0 ** (jnp.arange(0, ROTARY_DIM, 2, dtype=jnp.float32) / ROTARY_DIM)
            freqs = jnp.arange(T, dtype=jnp.float32)[:, None] * inv_freq[None, :]
            cos = jnp.cos(freqs)[None, :, None, :]
            sin = jnp.sin(freqs)[None, :, None, :]
            q1 = q[..., :half]
            q2 = q[..., half:ROTARY_DIM]
            rest = q[..., ROTARY_DIM:]
            return jnp.concatenate([q1 * cos - q2 * sin, q2 * cos + q1 * sin, rest], axis=-1)

        def segsum(x):
            T = x.shape[-1]
            xc = jnp.cumsum(x, axis=-1)
            ss = xc[..., :, None] - xc[..., None, :]
            mask = jnp.tril(jnp.ones((T, T), dtype=bool))
            return jnp.where(mask, ss, -jnp.inf)

        def ssd(x, dt, A, Bm, Cm):
            b, l, h, p = x.shape
            n = Bm.shape[-1]
            c = l // CHUNK
            xdt = (x * dt[..., None]).reshape(b, c, CHUNK, h, p)
            Adt = (dt * A).reshape(b, c, CHUNK, h).transpose(0, 3, 1, 2)
            Br = Bm.reshape(b, c, CHUNK, n)
            Cr = Cm.reshape(b, c, CHUNK, n)
            Acs = jnp.cumsum(Adt, axis=-1)
            Lmat = jnp.exp(segsum(Adt))
            Y_diag = jnp.einsum('bcln,bcsn,bhcls,bcshp->bclhp', Cr, Br, Lmat, xdt)
            decay_states = jnp.exp(Acs[..., -1:] - Acs)
            states = jnp.einsum('bcln,bhcl,bclhp->bchpn', Br, decay_states, xdt)
            A_chunk = jnp.pad(Acs[..., -1], ((0, 0), (0, 0), (1, 0)))
            decay_chunk = jnp.exp(segsum(A_chunk))
            states = jnp.concatenate([jnp.zeros_like(states[:, :1]), states], axis=1)
            new_states = jnp.einsum('bhzc,bchpn->bzhpn', decay_chunk, states)
            states_prev = new_states[:, :-1]
            Y_off = jnp.einsum('bcln,bchpn,bhcl->bclhp', Cr, states_prev, jnp.exp(Acs))
            return (Y_diag + Y_off).reshape(b, l, h, p)
        N, T, _ = x.shape
        qkv = (x @ W_in.T).reshape(N, T, 3, NHEAD, HEAD_DIM)
        q = apply_rope(qkv[:, :, 0]).reshape(N, T, D_MODEL)
        residual = q
        h = rmsnorm(q, norm_pre_w)
        zxbcdt = h @ W_zxbcdt.T
        z = zxbcdt[..., :D_INNER]
        xBC = zxbcdt[..., D_INNER:D_INNER + CONV_DIM]
        dt = jax.nn.softplus(zxbcdt[..., -H_SSM:] + dt_bias)
        xp = jnp.pad(xBC, ((0, 0), (D_CONV - 1, 0), (0, 0)))
        conv_out = conv_b
        for k in range(D_CONV):
            conv_out = conv_out + xp[:, k:k + T, :] * conv_w[:, k]
        xBC = jax.nn.silu(conv_out)
        x_ssm = xBC[..., :D_INNER].reshape(N, T, H_SSM, HEADDIM)
        Bm = xBC[..., D_INNER:D_INNER + D_STATE]
        Cm = xBC[..., D_INNER + D_STATE:]
        A = -jnp.exp(A_log)
        y = ssd(x_ssm, dt, A, Bm, Cm) + D_param[None, None, :, None] * x_ssm
        y = y.reshape(N, T, D_INNER)
        y = rmsnorm(y * jax.nn.silu(z), norm_gated_w)
        out = y @ W_out.T
        return out + residual

    def _L1_ffn_ref(x, wqkv, q_scale, k_scale, wo, ln_g, ln_b, w1, b1, w2, b2):
        import jax, jax.numpy as jnp
        import numpy as np
        DIM = 128
        DEPTH = 2
        HEADS = 8
        DIM_HEAD = 64
        WINDOW = 64
        INNER = HEADS * DIM_HEAD
        HID = int(DIM * 4 * 2 / 3)
        B, N = (2, 1024)
        QK_SCALE = 8.0

        def shift_token(t):
            t1, t2 = jnp.split(t, 2, axis=-1)
            t2 = jnp.pad(t2, ((0, 0), (1, 0), (0, 0)))[:, :-1]
            return jnp.concatenate([t1, t2], axis=-1)

        def l2norm(t):
            return t / jnp.clip(jnp.linalg.norm(t, axis=-1, keepdims=True), 1e-12)

        def rotate_half(x):
            x1, x2 = jnp.split(x, 2, axis=-1)
            return jnp.concatenate([-x2, x1], axis=-1)

        def rotary_xpos(q, k):
            n = q.shape[-2]
            half_idx = jnp.arange(0, DIM_HEAD, 2, dtype=jnp.float32)
            inv_freq = 1.0 / 10000.0 ** (half_idx / DIM_HEAD)
            t = jnp.arange(n, dtype=jnp.float32)
            freqs = t[:, None] * inv_freq[None, :]
            freqs = jnp.concatenate([freqs, freqs], axis=-1)
            base = (half_idx + 0.4 * DIM_HEAD) / (1.4 * DIM_HEAD)
            power = (t - n // 2) / float(WINDOW // 2)
            scale = base[None, :] ** power[:, None]
            scale = jnp.concatenate([scale, scale], axis=-1)
            cos, sin = (jnp.cos(freqs), jnp.sin(freqs))
            q = q * cos * scale + rotate_half(q) * sin * scale
            k = k * cos / scale + rotate_half(k) * sin / scale
            return (q, k)

        def local_attention(q, k, v):
            b, h, n, d = q.shape
            w = n // WINDOW
            bq = q.reshape(b, h, w, WINDOW, d) * QK_SCALE
            bk = k.reshape(b, h, w, WINDOW, d)
            bv = v.reshape(b, h, w, WINDOW, d)

            def look_around(t):
                p = jnp.pad(t, ((0, 0), (0, 0), (1, 0), (0, 0), (0, 0)))
                return jnp.concatenate([p[:, :, :w], p[:, :, 1:]], axis=3)
            bk, bv = (look_around(bk), look_around(bv))
            bt = jnp.arange(n).reshape(w, WINDOW)
            btp = jnp.pad(bt, ((1, 0), (0, 0)), constant_values=-1)
            btk = jnp.concatenate([btp[:w], btp[1:]], axis=1)
            sim = jnp.einsum('bhwid,bhwjd->bhwij', bq, bk)
            i = bt[:, :, None]
            j = btk[:, None, :]
            mask = (i < j) | (i > j + WINDOW) | (j == -1)
            sim = jnp.where(mask, -jnp.finfo(sim.dtype).max, sim)
            attn = jax.nn.softmax(sim, axis=-1)
            out = jnp.einsum('bhwij,bhwjd->bhwid', attn, bv)
            return out.reshape(b, h, n, d)

        def _layer(x, wqkv, qs, ksc, wo, lg, lb, w1, b1, w2, b2):
            b, n, _ = x.shape
            h = shift_token(x)
            qkv = h @ wqkv
            q, k, v = jnp.split(qkv, 3, axis=-1)
            to_heads = lambda t: t.reshape(b, n, HEADS, DIM_HEAD).transpose(0, 2, 1, 3)
            q, k, v = (to_heads(q), to_heads(k), to_heads(v))
            q = l2norm(q) * qs
            k = l2norm(k) * ksc
            q, k = rotary_xpos(q, k)
            o = local_attention(q, k, v)
            o = o.transpose(0, 2, 1, 3).reshape(b, n, INNER)
            x = x + o @ wo
            h = shift_token(x)
            mu = h.mean(-1, keepdims=True)
            var = h.var(-1, keepdims=True)
            h = (h - mu) / jnp.sqrt(var + 1e-05) * lg + lb
            h = h @ w1 + b1
            a, g = jnp.split(h, 2, axis=-1)
            h = a * jax.nn.gelu(g, approximate=False)
            x = x + h @ w2 + b2
            return x
        for l in range(DEPTH):
            x = _layer(x, wqkv[l], q_scale[l], k_scale[l], wo[l], ln_g[l], ln_b[l], w1[l], b1[l], w2[l], b2[l])
        return x
    x = L0_attn_x
    xn = _layernorm(x, axis=-1)
    s = _L0_attn_ref(xn, L0_attn_x_proj_w, L0_attn_dt_proj_w, L0_attn_dt_proj_b, L0_attn_A_log, L0_attn_D, L0_attn_x_proj_b_w, L0_attn_dt_proj_b_w, L0_attn_dt_proj_b_b, L0_attn_A_b_log, L0_attn_D_b)
    g = _silu(_L0_ffn_ref(xn, L0_ffn_router_w, L0_ffn_w1, L0_ffn_b1, L0_ffn_w2, L0_ffn_b2))
    x = x + s * g
    xn = _layernorm(x, axis=-1)
    s = _L1_attn_ref(xn, L1_attn_W_in, L1_attn_W_zxbcdt, L1_attn_conv_w, L1_attn_conv_b, L1_attn_dt_bias, L1_attn_A_log, L1_attn_D_param, L1_attn_norm_pre_w, L1_attn_norm_gated_w, L1_attn_W_out)
    g = _silu(_L1_ffn_ref(xn, L1_ffn_wqkv, L1_ffn_q_scale, L1_ffn_k_scale, L1_ffn_wo, L1_ffn_ln_g, L1_ffn_ln_b, L1_ffn_w1, L1_ffn_b1, L1_ffn_w2, L1_ffn_b2))
    x = x + s * g
    return x

_drawn_inputs = setup_inputs


def setup_inputs(seed=0):
    import zlib

    import numpy as np

    out = dict(_drawn_inputs(seed))
    spreads = {'L0_attn_D': (1.0, 0.6),
     'L0_attn_D_b': (1.0, 0.6),
     'L0_ffn_b1': (0.0, 0.337),
     'L0_ffn_b2': (0.0, 0.1),
     'L1_attn_conv_b': (0.0, 0.1),
     'L1_attn_norm_pre_w': (1.0, 0.2),
     'L1_attn_norm_gated_w': (1.0, 0.2),
     'L1_ffn_q_scale': (1.0, 0.6),
     'L1_ffn_k_scale': (1.0, 0.6),
     'L1_ffn_ln_g': (1.0, 0.6),
     'L1_ffn_ln_b': (0.0, 0.8),
     'L1_ffn_b1': (0.0, 0.8),
     'L1_ffn_b2': (0.0, 0.8)}
    factors = {'L0_attn_x_proj_w': 8.0,
     'L0_attn_dt_proj_w': 8.0,
     'L0_attn_dt_proj_b': 8.0,
     'L0_attn_A_log': 8.0,
     'L0_attn_x_proj_b_w': 8.0,
     'L0_attn_dt_proj_b_w': 8.0,
     'L0_attn_dt_proj_b_b': 8.0,
     'L0_attn_A_b_log': 8.0,
     'L0_ffn_router_w': 64.0,
     'L1_attn_dt_bias': 8.0,
     'L1_attn_A_log': 64.0,
     'L1_ffn_wqkv': 8.0,
     'L1_ffn_wo': 8.0,
     'L1_ffn_w1': 8.0,
     'L1_ffn_w2': 8.0}
    for name, (base, spread) in spreads.items():
        noise = np.random.default_rng([zlib.crc32(name.encode()), seed]).standard_normal(out[name].shape)
        drawn = base * np.exp(spread * noise) if base else spread * noise
        out[name] = jnp.asarray(drawn.astype(out[name].dtype))
    for name, factor in factors.items():
        out[name] = (out[name] * factor).astype(out[name].dtype)
    return out
```

```python
from contextlib import ExitStack

import numpy as np

import concourse.bass as bass
from concourse import mybir

F32 = mybir.dt.float32
BF16 = mybir.dt.bfloat16
I32 = mybir.dt.int32
ALU = mybir.AluOpType
ACT = mybir.ActivationFunctionType
AX = mybir.AxisListType

NB, T, D = 16, 512, 128
P = 128
NT = T // P
NS, RK = 16, 32
FH = 512
NE = 8
HM, PM, DI = 4, 64, 256
TAPS = 4
HA, DH, INNER = 8, 64, 512
WIN = 64
HID = 341
HT = [(0, 128), (128, 128), (256, HID - 256)]
NL = 2
EPS = 1e-5
MASKED = -1e30

WIDTHS = [("wdelta", 2 * RK), ("wbc", 2 * 96), ("dtw", D), ("dtb", 2), ("Dfb", 2), ("b1", 4), ("b2", 1),
          ("alog", 2 * NS), ("router", NE), ("w1", FH), ("w2", 4 * D),
          ("mwq", D), ("mwqr", D), ("mwz", DI), ("mwc", 512), ("mwdt", HM), ("convb", 4), ("mD", 2),
          ("npre", 1), ("ngate", 2), ("wout", 2 * D)]
for _l in range(NL):
    WIDTHS += [(f"wq{_l}", INNER), (f"wqr{_l}", INNER), (f"wk{_l}", INNER), (f"wkr{_l}", INNER),
               (f"wv{_l}", INNER), (f"wo{_l}", 4 * D), (f"w1_{_l}", 2 * HID), (f"w2_{_l}", 3 * D),
               (f"fb1_{_l}", 6), (f"fb2_{_l}", 1), (f"lg{_l}", 1), (f"lb{_l}", 1), (f"qs{_l}", 4)]
CWIDTHS = [("ident", P), ("tri", P), ("lastrow", P), ("headsum", 2), ("selbase", 32),
           ("mcos", T), ("msin", T)]
TABLES = ("cosq", "sinq", "cosk", "sink")


def offsets(widths):
    at, out = 0, {}
    for name, n in widths:
        out[name] = (at, n)
        at += n
    return out, at


WOFF, WCOLS = offsets(WIDTHS)
COFF, CCOLS = offsets(CWIDTHS)

A_JOBS = ([("xT", "a_xT", 1), ("mean", "a_xc", 1), ("var", "a_ln", 1), ("dlow", "a_dlow", 1),
           ("bc0", "a_bcr", 1), ("bc1", "a_bcr", 2), ("z0", "a_zrel", 1), ("z1", "a_zrel", 2), ("router", "a_rd", 1)]
          + [(f"up{m}", "a_h1", m + 1) for m in range(4)] + [("rbc", "a_rbc", 1)]
          + [job for k in range(2 * NS) for job in ((f"B{k}", "a_bx", k + 1), (f"C{k}", "a_Cs", k + 1))])
B_JOBS = ([("mean", "m_xc", 1), ("var", "m_ln", 1), ("mq", "m_t1", 1), ("mqr", "m_t2", 1), ("mss", "m_qln", 1)]
          + [(f"cx{t}", "m_xs", t + 1) for t in range(4)] + [(f"mz{t}", "m_sz", t + 1) for t in range(2)]
          + [("mdt", "m_dtz", 1), ("acs", "m_acs", 1), ("acl", "m_dlast", 1), ("ab0", "m_ld", 1)]
          + [(f"ab{q}", "m_ea", q) for q in range(1, NT)]
          + [("G", "m_G", 1), ("bt", "m_bt", 1), ("xt0", "m_xdt", 1), ("xt1", "m_xdt", 2)]
          + [(f"st{q}", "m_st", q + 1) for q in range(NT - 1)]
          + [("y0", "m_y2", 1), ("y1", "m_y2", 2), ("yss", "m_yln", 1), ("mo", "m_sm1", 1)])
UNITS = [(q, g) for q in range(NT) for g in range(HA // 2)]
NU = len(UNITS)
LAG_T, LAG_V = 2, 3
for _l in range(NL):
    for _m in range(4):
        B_JOBS += [(f"{_k}{_l}{_m}", _s, 4 * _l + _m + 1)
                   for _k, _s in (("q", "t_qc"), ("qr", "t_qr"), ("k", "t_kc"), ("kr", "t_kr"))]
    B_JOBS += [(f"nrm{_l}", "t_nrm", _l + 1)] + [(f"v{_l}{_q}", "t_v", 4 * _l + _q + 1) for _q in range(NT)]
    B_JOBS += [(f"vh{_l}{_q}", "t_vh", 3 * _l + _q) for _q in range(1, NT)]
    B_JOBS += [(f"rk{_l}{_m}", "t_k", 4 * _l + _m + 1) for _m in range(4)]
    for _n in range(NU + LAG_V + 1):
        if _n < NU:
            B_JOBS += [(f"S{_l}_{_n}", "t_P", NU * _l + _n + 1)]
        if LAG_T <= _n < NU + LAG_T:
            B_JOBS += [(f"PT{_l}_{_n - LAG_T}", "t_PT", NU * _l + _n - LAG_T + 1)]
        if _n > LAG_V and (_n - LAG_V) % 4 == 0:
            B_JOBS += [(f"oT{_l}{(_n - LAG_V) // 4 - 1}", "t_oT", 4 * _l + (_n - LAG_V) // 4)]
    B_JOBS += [(f"wo{_l}", "f_xa", _l + 1), (f"lmean{_l}", "f_xc", _l + 1), (f"lvar{_l}", "f_ln", _l + 1)]
    for _m in range(3):
        B_JOBS += [(f"fg{_l}{_m}", "f_gl", 3 * _l + _m + 1), (f"fa{_l}{_m}", "f_ha", 3 * _l + _m + 1)]
    B_JOBS += [(f"fd{_l}", "f_y", _l + 1)]
B_JOBS += [("xo", "xo", 1)]

SCAN = 9
A_END = SCAN + 2 * NS
A_SLOTS = A_END + 1
LAYER = 16
UNIT = 8
UNITS_END = UNIT + NU + LAG_V + 1
LAYER_SLOTS = UNITS_END + 5
B_END = LAYER + NL * LAYER_SLOTS
B_SLOTS = B_END + 2

PER = dict(load=16, store=16, a_mid=2, a_bch=2, a_bcr=2, a_zabs=2, a_zrel=2, a_top=4, a_h1=4, a_down=4,
           a_dA=2 * NS, a_Cs=2 * NS, a_bx=2 * NS, a_h=2 * NS, a_hc=2 * NS, a_yacc=2 * NS,
           m_xs=4, m_sz=2, m_ea=3, m_ld=4, m_L=4, m_M=4, m_Ce=3, m_xdt=2, m_sttmp=2, m_st=3, m_y2=2, m_y3=2,
           m_ysq=2, t_xs=2 * NL, f_xs=2 * NL, t_nrm=NL, t_clip=NL, t_rqk=NL, t_rq8=NL, t_vh=3 * NL, t_vo=3 * NL, t_S0=NU * NL,
           t_max=NU * NL, t_bias=NU * NL, t_P=NU * NL, t_PT=NU * NL, t_O=NU * NL, f_gl=3 * NL, f_ha=3 * NL)
for _s in ("t_qc", "t_qr", "t_kc", "t_kr", "t_qsq", "t_ksq", "t_q", "t_ksum", "t_k", "t_v", "t_rinv", "t_on", "t_oT"):
    PER[_s] = 4 * NL
for _s in ("f_xa", "f_xc", "f_sq", "f_ln", "f_r", "f_xr", "f_hn", "f_y"):
    PER[_s] = NL


def build(nc, x, wpack, cpack, mask, tables, taps, rowpack, out):
    ctx = ExitStack()
    with ctx:
        def sb(name, shape, dt=F32):
            return ctx.enter_context(nc.sbuf_tensor(name, [P] + shape, dt))

        sems = {}

        def sem(name):
            if name not in sems:
                sems[name] = ctx.enter_context(nc.semaphore(name))
            return sems[name]

        def step(name, i, k=None):
            per = PER.get(name, 1)
            return sem(name), i * per + (per if k is None else k)

        def later(i):
            return not isinstance(i, int) or i > 0

        def before(name, i, k=None):
            per = PER.get(name, 1)
            return sem(name), i * per + ((per if k is None else k) - per)

        banks = [ctx.enter_context(nc.psum_tensor(f"bank{b}", [P, 512], F32)) for b in range(8)]
        y_acc, o_acc = banks[2], banks[7]
        rings = {"A": (banks[0:2], A_JOBS), "B": (banks[3:7], B_JOBS)}

        def place(ring, job):
            bs, jobs = rings[ring]
            n = [j[0] for j in jobs].index(job)
            b = n % len(bs)
            return bs[b], b, n // len(bs), len(range(b, len(jobs), len(bs)))

        def bank(ring, job):
            return place(ring, job)[0]

        def reader(ring, job):
            bs, jobs = rings[ring]
            n = [j[0] for j in jobs].index(job)
            if n >= len(bs):
                return jobs[n - len(bs)], False
            return jobs[n + (len(jobs) - 1 - n) // len(bs) * len(bs)], True

        def used(ring, job, i):
            return later(i) or not reader(ring, job)[1]

        def vacant(ring, job, i):
            (_, name, k), earlier = reader(ring, job)
            return before(name, i, k) if earlier else step(name, i, k)

        def full(ring, job):
            return sem(f"{ring}bank{place(ring, job)[1]}_full")

        def filled(ring, job, i):
            _, b, k, per = place(ring, job)
            return sem(f"{ring}bank{b}_full"), i * per + k + 1

        W = sb("W", [WCOLS])
        C = sb("C", [CCOLS])

        def w(name, a=0, b=None, rows=slice(0, P)):
            at, n = WOFF[name]
            return W[rows, at + a:at + (n if b is None else b)]

        def c(name, a=0, b=None, rows=slice(0, P)):
            at, n = COFF[name]
            return C[rows, at + a:at + (n if b is None else b)]

        ident = c("ident")
        rows_b = sb("rows_b", [2 * 16])
        inv128 = sb("inv128", [P])
        inv256 = sb("inv256", [P])
        col_eps = sb("col_eps", [1])
        col_one = sb("col_one", [1])
        ident16 = sb("ident16", [P], BF16)
        mask16 = sb("mask16", [384], BF16)
        sel16 = sb("sel16", [32], BF16)
        neg_a = sb("neg_a", [2 * NS])
        dsum = sb("dsum", [1])
        wz_f, wdt_f = w("mwz"), w("mwdt")
        wout_f = w("wout").rearrange("p (g n) -> p g n", g=2)
        wc_f = sb("wc_f", [TAPS, 512])
        neg_am = sb("neg_am", [16])
        rot = sb("rot", [NL, 4, T])
        x_tok = sb("x_tok", [NT, D])
        xT = sb("xT", [T])
        xc = sb("xc", [T])
        xsq = sb("xsq", [T])
        xn = sb("xn", [T])
        dlow = sb("dlow", [T])
        parts = sb("parts", [2, T], BF16)
        rt = sb("rt", [4, NT, NE])
        rs = sb("rs", [6, NT])
        rw = sb("rw", [NT, 2])
        gate = sb("gate", [T])
        delta = sb("delta", [2, T])
        u = sb("u", [2, T])
        zmask = u[:, :, :].bitcast(I32)
        x1 = sb("x1", [T])
        dA, Cs, bx, hst, hc = [sb(name, [2, T]) for name in ("dA", "Cs", "bx", "hst", "hc")]
        ez, zrel, zp, h1, bcr = dA, Cs, bx, hst, hc
        rstd, fo, ys, rbc = xsq, xc, xsq, dlow
        x1b = sb("x1b", [T])
        xn2 = sb("xn2", [T])
        rsB = sb("rsB", [T])
        xs0 = sb("xs0", [T + 1])
        hpad = sb("hpad", [T + 3])
        mq = sb("mq", [T])
        dtk = sb("dtk", [10, 16])
        dtm = sb("dtm", [16], I32)
        dt = sb("dt", [16])
        dta = sb("dta", [16])
        acs = sb("acs", [16])
        dlast = sb("dlast", [16])
        decay = sb("decay", [16])
        etot = sb("etot", [16])
        sm = sb("sm", [T])
        tmp1 = sb("tmp1", [2, T])
        tmp2 = sb("tmp2", [2, T])
        nrm = sb("nrm", [3, 64])
        rq8 = sb("rq8", [32])
        mx = sb("mx", [4, 2])
        bias = sb("bias", [4, 2])
        rsum = sb("rsum", [2, 4, 2])
        rinv = sb("rinv", [2, 8])
        xa = sb("xa", [T])
        yB = sb("yB", [T])
        sqk = sb("sqk", [2, 4, T])
        qk = sb("qk", [2, 4, T])
        vt = sb("vt", [NT, INNER])
        vbd = sb("vbd", [3, 4, P])
        Pm = sb("Pm", [3, 384])
        PT = sb("PT", [2, 384])
        on = sb("on", [2, INNER])
        oT = sqk[:, 1]
        xsA, x2, xo = xs0, x1b, xa
        gl = on
        big1 = sqk[:, 0].rearrange("p q (h l) -> p q h l", h=HM)
        big2 = sqk[:, 1].rearrange("p q (h l) -> p q h l", h=HM)
        xbc = qk[:, 0]
        xdt = qk[:, 1, 0:2].rearrange("p a (b h d) -> p (a b) h d", b=2, h=HM)
        xdd = qk[:, 1, 2:4].rearrange("p a (b h d) -> p (a b) h d", b=2, h=HM)
        sz, y3 = vt[:, 0:2], vt[:, 2:4]
        pmf = Pm[:, :, :].rearrange("p a b -> p (a b)")
        btok = pmf[:, 0:T].rearrange("p (q n) -> p q n", q=NT)
        Gm = pmf[:, T:2 * T].rearrange("p (q n) -> p q n", q=NT)
        onf = on[:, :, :].rearrange("p a b -> p (a b)")
        st = onf[:, 0:768].rearrange("p (q h d) -> p q h d", q=3, h=HM)
        sttmp = onf[:, 768:1024].rearrange("p (h d) -> p h d", h=HM)

        dtb_row = rows_b[:, 0:16]
        alog_row = rows_b[:, 16:32]

        def over(ap, n):
            return ap.unsqueeze(2).to_broadcast([ap.shape[0], ap.shape[1], n])

        def each(ap, n):
            return ap.unsqueeze(1).to_broadcast([ap.shape[0], n, ap.shape[1]])

        def wait_alone(e, name, i, k=None):
            per = PER.get(name, 1)
            value = i * per + (per if k is None else k)
            if not isinstance(i, int):
                value = e.snap(value)
            e.wait_ge(sem("setup"), SETUP)
            e.wait_ge(sem(name), value)

        x_v = x.rearrange("b (q p) d -> b p q d", p=P)
        out_v = out.rearrange("b (q p) d -> b p q d", p=P)

        def share(stage):
            at = [next(stage)]

            def upto(slot):
                while at[0] <= slot:
                    at[0] = next(stage, B_SLOTS)
            return upto

        def both(stage_a, stage_b):
            a, b = share(stage_a), share(stage_b)
            for slot in range(B_SLOTS):
                b(slot)
                a((slot + 1) * A_SLOTS // B_SLOTS - 1)

        def alone(stage):
            share(stage)(B_SLOTS - 1)

        def run(e, stage_a, stage_b):
            alone(stage_a(0))
            both(stage_a(1), stage_b(0))
            with e.Fori(2, NB) as i:
                both(stage_a(i), stage_b(e.snap(i - 1)))
            alone(stage_b(NB - 1))

        block = ctx.enter_context(nc.Block())

        @block.sync
        def _(sp):
            sp.dma_start(W[:, :], wpack).then_inc(sem("weights"), 16)
            sp.dma_start(C[:, :], cpack).then_inc(sem("consts"), 16)
            sp.dma_start(Pm[:, 0, :], mask).then_inc(sem("mask"), 16)
            for l in range(NL):
                sp.dma_start(rot[:, l], tables.rearrange("n p t -> p n t")).then_inc(sem("tables"), 16)
            sp.dma_start(wc_f[:, :, :], taps.partition_broadcast(P)).then_inc(sem("taps"), 16)
            sp.dma_start(rows_b[:, :], rowpack.partition_broadcast(P)).then_inc(sem("rows"), 16)

            def stage_a(i):
                yield 0
                if later(i):
                    sp.wait_ge(*before("a_xT", i))
                src = x_v[i] if isinstance(i, int) else x_v[bass.ds(i, 1)].rearrange("b p q d -> (b p) q d")
                sp.dma_start(x_tok[:, :, :], src).then_inc(sem("load"), 16)

            def stage_b(i):
                yield B_END + 1
                sp.wait_ge(*step("xo", i))
                dst = out_v[i] if isinstance(i, int) else out_v[bass.ds(i, 1)].rearrange("b p q d -> (b p) q d")
                sp.dma_start(dst, xo[:, :].rearrange("p (q d) -> p q d", q=NT)).then_inc(sem("store"), 16)

            run(sp, stage_a, stage_b)
            sp.wait_ge(sem("store"), NB * 16)

        @block.tensor
        def _(pe):
            mm = nc.tensor.matmul
            pe.wait_ge(sem("setup"), SETUP)

            def stage_a(i):
                pe.wait_ge(*step("load", i))
                if used("A", "xT", i):
                    pe.wait_ge(*vacant("A", "xT", i))
                b = bank("A", "xT")
                for q in range(NT):
                    last = nc.tensor.transpose(b[:, q * P:(q + 1) * P], x_tok[:, q, :], ident)
                last.then_inc(full("A", "xT"), 1)
                yield 1
                pe.wait_ge(*step("a_xT", i))
                if used("A", "mean", i):
                    pe.wait_ge(*vacant("A", "mean", i))
                b = bank("A", "mean")
                mm(b[:, :], inv128[:, :], xT[:, :], start=True, stop=True).then_inc(full("A", "mean"), 1)
                yield 2
                pe.wait_ge(*step("a_xsq", i))
                if used("A", "var", i):
                    pe.wait_ge(*vacant("A", "var", i))
                b = bank("A", "var")
                mm(b[:, :], inv128[:, :], xsq[:, :], start=True, stop=True).then_inc(full("A", "var"), 1)
                yield 3
                pe.wait_ge(*step("a_xn", i))
                if used("A", "dlow", i):
                    pe.wait_ge(*vacant("A", "dlow", i))
                b = bank("A", "dlow")
                mm(b[0:64, :], w("wdelta"), xn[:, :], start=True, stop=True).then_inc(full("A", "dlow"), 1)
                for d in range(2):
                    if used("A", f"bc{d}", i):
                        pe.wait_ge(*vacant("A", f"bc{d}", i))
                    b = bank("A", f"bc{d}")
                    mm(b[0:96, :], w("wbc", 96 * d, 96 * d + 96), xn[:, :],
                       start=True, stop=True).then_inc(full("A", f"bc{d}"), 1)
                yield 4
                pe.wait_ge(*step("a_dlow", i))
                for d in range(2):
                    r = slice(RK * d, RK * d + RK)
                    if used("A", f"z{d}", i):
                        pe.wait_ge(*vacant("A", f"z{d}", i))
                    b = bank("A", f"z{d}")
                    mm(b[:, :], w("dtw", rows=r), dlow[r, :], start=True, stop=True).then_inc(full("A", f"z{d}"), 1)
                if used("A", "router", i):
                    pe.wait_ge(*vacant("A", "router", i))
                b = bank("A", "router")
                for q in range(NT):
                    last = mm(b[:, q * NE:(q + 1) * NE], xn[:, q * P:(q + 1) * P], w("router"), start=True, stop=True)
                last.then_inc(full("A", "router"), 1)
                def down(m):
                    pe.wait_ge(*step("a_h1", i, m + 1))
                    if m == 0:
                        if later(i):
                            pe.wait_ge(*before("a_y", i))
                    mm(y_acc[:, :], w("w2", m * D, m * D + D), h1[:, m % 2, :], start=(m == 0), stop=(m == 3))\
                        .then_inc(sem("a_down"), 1)

                yield 5
                for m in range(4):
                    if m == 2:
                        yield 6
                    if used("A", f"up{m}", i):
                        pe.wait_ge(*vacant("A", f"up{m}", i))
                    b = bank("A", f"up{m}")
                    mm(b[:, :], w("w1", m * P, m * P + P), xn[:, :], start=True, stop=True)\
                        .then_inc(full("A", f"up{m}"), 1)
                    if m > 0:
                        down(m - 1)
                yield 7
                down(3)
                pe.wait_ge(*step("a_rfac", i))
                if used("A", "rbc", i):
                    pe.wait_ge(*vacant("A", "rbc", i))
                b = bank("A", "rbc")
                for q in range(NT):
                    last = mm(b[:, q * P:(q + 1) * P], rs[:, 5, q:q + 1].to_broadcast([P, P]), ident,
                              start=True, stop=True)
                last.then_inc(full("A", "rbc"), 1)

                def accumulate(k):
                    pe.wait_ge(*step("a_hc", i, k + 1))
                    if k == 0:
                        pe.wait_ge(*step("a_fo", i))
                    mm(y_acc[:, :], ident, hc[:, k % 2, :], start=(k == 0), stop=(k == 2 * NS - 1))\
                        .then_inc(sem("a_yacc"), 1)

                yield SCAN
                pe.wait_ge(*step("a_parts", i))
                for k in range(2 * NS):
                    yield SCAN + k
                    d, s = k // NS, k % NS
                    for name, o in (("B", 0), ("C", NS)):
                        if used("A", f"{name}{k}", i):
                            pe.wait_ge(*vacant("A", f"{name}{k}", i))
                        b = bank("A", f"{name}{k}")
                        mm(b[:, :], sel16[0:96, o + s:o + s + 1].to_broadcast([96, P]), parts[0:96, d, :], start=True, stop=True)\
                            .then_inc(full("A", f"{name}{k}"), 1)
                    if k >= 2:
                        accumulate(k - 2)
                yield A_END
                accumulate(2 * NS - 2)
                accumulate(2 * NS - 1)

            def norm_sum(ring, job, i, weights, rhs):
                if used(ring, job, i):
                    pe.wait_ge(*vacant(ring, job, i))
                b = bank(ring, job)
                mm(b[:, :], weights, rhs, start=True, stop=True).then_inc(full(ring, job), 1)

            def stage_b(i):
                pe.wait_ge(*step("m_x1b", i))
                norm_sum("B", "mean", i, inv128[:, :], x1b[:, :])
                yield 1
                pe.wait_ge(*step("m_xsq", i))
                norm_sum("B", "var", i, inv128[:, :], tmp2[:, 0, :])
                yield 2
                pe.wait_ge(*step("m_xn", i))
                norm_sum("B", "mq", i, w("mwq"), xn2[:, :])
                norm_sum("B", "mqr", i, w("mwqr"), xn2[:, :])
                yield 3
                pe.wait_ge(*step("m_qsq", i))
                norm_sum("B", "mss", i, inv128[:, :], tmp2[:, 0, :])
                pe.wait_ge(*step("m_h", i))
                for t in range(4):
                    yield 4 + t // 2
                    if used("B", f"cx{t}", i):
                        pe.wait_ge(*vacant("B", f"cx{t}", i))
                    b = bank("B", f"cx{t}")
                    for k in range(TAPS):
                        last = mm(b[:, :], wc_f[:, k, t * P:(t + 1) * P], hpad[:, k:k + T],
                                  start=(k == 0), stop=(k == TAPS - 1))
                    last.then_inc(full("B", f"cx{t}"), 1)
                for t in range(2):
                    norm_sum("B", f"mz{t}", i, wz_f[:, t * P:(t + 1) * P], hpad[:, 3:3 + T])
                yield 6
                if used("B", "mdt", i):
                    pe.wait_ge(*vacant("B", "mdt", i))
                b = bank("B", "mdt")
                for q in range(NT):
                    last = mm(b[:, q * HM:(q + 1) * HM], hpad[:, 3 + q * P:3 + (q + 1) * P], wdt_f[:, :],
                              start=True, stop=True)
                last.then_inc(full("B", "mdt"), 1)
                yield 8
                pe.wait_ge(*step("m_dta", i))
                if used("B", "acs", i):
                    pe.wait_ge(*vacant("B", "acs", i))
                b = bank("B", "acs")
                mm(b[:, 0:16], c("tri"), dta[:, :], start=True, stop=True).then_inc(full("B", "acs"), 1)
                yield 9
                pe.wait_ge(*step("m_acs", i))
                if used("B", "acl", i):
                    pe.wait_ge(*vacant("B", "acl", i))
                b = bank("B", "acl")
                mm(b[:, 0:16], c("lastrow"), acs[:, :], start=True, stop=True).then_inc(full("B", "acl"), 1)
                for q in range(NT):
                    yield 9 + q // 2
                    if used("B", f"ab{q}", i):
                        pe.wait_ge(*vacant("B", f"ab{q}", i))
                    b = bank("B", f"ab{q}")
                    for h in range(HM):
                        n = q * HM + h
                        last = mm(b[:, h * P:(h + 1) * P], acs[:, n:n + 1].to_broadcast([P, P]), ident,
                                  start=True, stop=True)
                    last.then_inc(full("B", f"ab{q}"), 1)
                yield 11
                pe.wait_ge(*step("m_xs", i))
                if used("B", "G", i):
                    pe.wait_ge(*vacant("B", "G", i))
                b = bank("B", "G")
                for q in range(NT):
                    ts = slice(q * P, (q + 1) * P)
                    last = mm(b[:, ts], xbc[:, 2, ts], xbc[:, 3, ts], start=True, stop=True)
                last.then_inc(full("B", "G"), 1)
                for job, t in (("bt", 2), ("xt0", 0), ("xt1", 1)):
                    if job == "xt0":
                        yield 12
                    if used("B", job, i):
                        pe.wait_ge(*vacant("B", job, i))
                    b = bank("B", job)
                    for q in range(NT):
                        last = nc.tensor.transpose(b[:, q * P:(q + 1) * P], xbc[:, t, q * P:(q + 1) * P], ident)
                    last.then_inc(full("B", job), 1)
                yield 13
                pe.wait_ge(*step("m_bt", i))
                pe.wait_ge(*step("m_xdd", i))
                for q in range(3):
                    if used("B", f"st{q}", i):
                        pe.wait_ge(*vacant("B", f"st{q}", i))
                    b = bank("B", f"st{q}")
                    mm(b[:, 0:256], btok[:, q, :], xdd[:, q, :, :], start=True, stop=True)\
                        .then_inc(full("B", f"st{q}"), 1)
                yield 14
                pe.wait_ge(*step("m_M", i))
                pe.wait_ge(*step("m_Ce", i))
                pe.wait_ge(*step("m_st", i))
                for g in range(2):
                    if used("B", f"y{g}", i):
                        pe.wait_ge(*vacant("B", f"y{g}", i))
                    b = bank("B", f"y{g}")
                    for q in range(NT):
                        for hh in range(2):
                            h = 2 * g + hh
                            dst = b[hh * PM:(hh + 1) * PM, q * P:(q + 1) * P]
                            last = mm(dst, xdt[:, q, h, :], big2[:, q, h, :], start=True, stop=(q == 0))
                            if q > 0:
                                last = mm(dst, st[:, q - 1, h, :], big1[:, q, h, :], start=False, stop=True)
                    last.then_inc(full("B", f"y{g}"), 1)
                yield 15
                if used("B", "yss", i):
                    pe.wait_ge(*vacant("B", "yss", i))
                b = bank("B", "yss")
                for g in range(2):
                    pe.wait_ge(*step("m_ysq", i, g + 1))
                    last = mm(b[:, :], inv256[:, :], tmp2[:, g, :], start=(g == 0), stop=(g == 1))
                last.then_inc(full("B", "yss"), 1)
                if used("B", "mo", i):
                    pe.wait_ge(*vacant("B", "mo", i))
                b = bank("B", "mo")
                for g in range(2):
                    last = mm(b[:, :], wout_f[:, g, :], y3[:, g, :], start=(g == 0), stop=(g == 1))
                last.then_inc(full("B", "mo"), 1)

                for l in range(NL):
                    xsh = xs0
                    at_l = LAYER + l * LAYER_SLOTS
                    yield at_l
                    pe.wait_ge(*step("t_xs", i, 2 * l + 2))
                    for m in range(4):
                        yield at_l + m
                        for kind in ("q", "qr", "k", "kr"):
                            norm_sum("B", f"{kind}{l}{m}", i, w(f"w{kind}{l}", m * P, m * P + P), xsh[:, 0:T])
                    yield at_l + 4
                    if used("B", f"nrm{l}", i):
                        pe.wait_ge(*vacant("B", f"nrm{l}", i))
                    b = bank("B", f"nrm{l}")
                    pe.wait_ge(*step("t_qsq", i, 4 * l + 4))
                    pe.wait_ge(*step("t_ksq", i, 4 * l + 4))
                    for kind in range(2):
                        for q in range(NT):
                            for m in range(4):
                                at = 32 * kind + 8 * q + 2 * m
                                last = mm(b[:, at:at + 2], sqk[:, kind, m, q * P:(q + 1) * P], c("headsum"),
                                          start=True, stop=True)
                    last.then_inc(full("B", f"nrm{l}"), 1)
                    for q in range(NT):
                        yield at_l + 4 + q // 2
                        if used("B", f"v{l}{q}", i):
                            pe.wait_ge(*vacant("B", f"v{l}{q}", i))
                        b = bank("B", f"v{l}{q}")
                        mm(b[:, :], xsh[:, q * P:(q + 1) * P], w(f"wv{l}"), start=True, stop=True)\
                            .then_inc(full("B", f"v{l}{q}"), 1)
                    for q in range(1, NT):
                        yield at_l + 5 + q // 2
                        if used("B", f"vh{l}{q}", i):
                            pe.wait_ge(*vacant("B", f"vh{l}{q}", i))
                        b = bank("B", f"vh{l}{q}")
                        even = w(f"wv{l}").rearrange("p (g two d) -> p g two d", two=2, d=DH)[:, :, 0, :]
                        mm(b[0:WIN, 0:256], xsh[:, q * P - WIN:q * P], even, start=True, stop=True)\
                            .then_inc(full("B", f"vh{l}{q}"), 1)
                    pe.wait_ge(*step("t_rqk", i, l + 1))
                    for m in range(4):
                        yield at_l + 6 + m // 2
                        if used("B", f"rk{l}{m}", i):
                            pe.wait_ge(*vacant("B", f"rk{l}{m}", i))
                        b = bank("B", f"rk{l}{m}")
                        for q in range(NT):
                            for hh in range(2):
                                at = 32 + 8 * q + 2 * m + hh
                                last = mm(b[hh * DH:(hh + 1) * DH, q * P:(q + 1) * P],
                                          nrm[:, 2, at:at + 1].to_broadcast([P, DH]), ident, start=True, stop=True)
                        last.then_inc(full("B", f"rk{l}{m}"), 1)
                    yield at_l + UNIT
                    pe.wait_ge(*step("t_q", i, 4 * l + 4))
                    pe.wait_ge(*step("t_k", i, 4 * l + 4))

                    def scores(n, hh):
                        q, g = UNITS[n]
                        qs = slice(q * P, (q + 1) * P)
                        r = slice(hh * DH, (hh + 1) * DH)
                        if hh == 0:
                            if reader("B", f"S{l}_{n}")[0][1] != "t_k":
                                pe.wait_ge(*vacant("B", f"S{l}_{n}", i))
                            b = bank("B", f"S{l}_{n}")
                            if q == 0:
                                for at in (0, P):
                                    mm(b[:, at:at + P], ident16[:, :], mask16[:, 0:P], start=(at == 0), stop=False,
                                       skip_group_check=True)
                            else:
                                mm(b[:, 0:384], ident16[:, :], mask16[:, :], start=True, stop=False,
                                   skip_group_check=True)
                        else:
                            b = bank("B", f"S{l}_{n}")
                            pe.wait_ge(*step("t_S0", i, NU * l + n + 1))
                        cur, prev = ((0, 128), (P if q == 0 else 256, 192))[hh]
                        last = mm(b[:, cur:cur + P], qk[r, 0, g, qs], qk[r, 1, g, qs], start=False, stop=(q == 0),
                                  skip_group_check=True)
                        if q > 0:
                            last = mm(b[:, prev:prev + WIN], qk[r, 0, g, qs], qk[r, 1, g, q * P - WIN:q * P],
                                      start=False, stop=True, skip_group_check=True)
                        last.then_inc(full("B", f"S{l}_{n}") if hh else sem("t_S0"), 1)

                    def turn(n):
                        q, g = UNITS[n]
                        pe.wait_ge(*step("t_P", i, NU * l + n + 1))
                        if used("B", f"PT{l}_{n}", i):
                            pe.wait_ge(*vacant("B", f"PT{l}_{n}", i))
                        b = bank("B", f"PT{l}_{n}")
                        for m in range(2 if q == 0 else 3):
                            last = nc.tensor.transpose(b[:, m * P:(m + 1) * P], Pm[:, n % 3, m * P:(m + 1) * P], ident)
                        last.then_inc(full("B", f"PT{l}_{n}"), 1)

                    def weigh(n):
                        q, g = UNITS[n]
                        pe.wait_ge(*step("t_PT", i, NU * l + n + 1))
                        if g == 0:
                            if l == 0 and q == 0:
                                if later(i):
                                    pe.wait_ge(*before("t_on", i))
                            elif l or q:
                                pe.wait_ge(*step("t_on", i, 4 * l + q))
                        p = PT[:, n % 2, :]
                        he, ho = 2 * g, 2 * g + 1
                        de = o_acc[:, he * DH:(he + 1) * DH]
                        do = o_acc[:, ho * DH:(ho + 1) * DH]
                        last = mm(de, p[:, 0:P], vt[:, q, he * DH:(he + 1) * DH], start=True, stop=(q == 0),
                                  skip_group_check=True)
                        if q == 0:
                            last = mm(do, p[:, P:2 * P], vt[:, q, ho * DH:(ho + 1) * DH], start=True, stop=True)
                        else:
                            mm(do, p[:, 2 * P:3 * P], vt[:, q, ho * DH:(ho + 1) * DH], start=False, stop=False,
                               skip_group_check=True)
                            last = mm(o_acc[:, he * DH:(ho + 1) * DH], p[:, P:2 * P], vbd[:, q - 1, g, :],
                                      start=False, stop=True, skip_group_check=True)
                        last.then_inc(sem("t_O"), 1)

                    pe.wait_ge(*step("t_v", i, 4 * l + 4))
                    pe.wait_ge(*step("t_vo", i, 3 * l + 3))
                    for n in range(NU + LAG_V + 1):
                        yield at_l + UNIT + n
                        if n < NU:
                            scores(n, 0)
                        if LAG_T <= n < NU + LAG_T:
                            turn(n - LAG_T)
                        if n > LAG_V and (n - LAG_V) % 4 == 0:
                            q = (n - LAG_V) // 4 - 1
                            pe.wait_ge(*step("t_on", i, 4 * l + q + 1))
                            if used("B", f"oT{l}{q}", i):
                                pe.wait_ge(*vacant("B", f"oT{l}{q}", i))
                            b = bank("B", f"oT{l}{q}")
                            for m in range(4):
                                last = nc.tensor.transpose(b[:, m * P:(m + 1) * P], on[:, q % 2, m * P:(m + 1) * P],
                                                           ident)
                            last.then_inc(full("B", f"oT{l}{q}"), 1)
                        if n < NU:
                            scores(n, 1)
                        if LAG_V <= n < NU + LAG_V:
                            weigh(n - LAG_V)
                    yield at_l + UNITS_END
                    pe.wait_ge(*step("t_oT", i, 4 * l + 4))
                    if used("B", f"wo{l}", i):
                        pe.wait_ge(*vacant("B", f"wo{l}", i))
                    b = bank("B", f"wo{l}")
                    for m in range(4):
                        last = mm(b[:, :], w(f"wo{l}", m * D, m * D + D), oT[:, m, :], start=(m == 0), stop=(m == 3))
                    last.then_inc(full("B", f"wo{l}"), 1)
                    yield at_l + UNITS_END + 1
                    pe.wait_ge(*step("f_xs", i, 2 * l + 2))
                    norm_sum("B", f"lmean{l}", i, inv128[:, :], xsA[:, 0:T])
                    yield at_l + UNITS_END + 2
                    pe.wait_ge(*step("f_sq", i, l + 1))
                    norm_sum("B", f"lvar{l}", i, inv128[:, :], tmp2[:, 0, :])
                    yield at_l + UNITS_END + 3
                    pe.wait_ge(*step("f_hn", i, l + 1))
                    for m, (at, n) in enumerate(HT):
                        for kind, o in (("fg", HID), ("fa", 0)):
                            if used("B", f"{kind}{l}{m}", i):
                                pe.wait_ge(*vacant("B", f"{kind}{l}{m}", i))
                            b = bank("B", f"{kind}{l}{m}")
                            mm(b[0:n, :], w(f"w1_{l}", o + at, o + at + n), tmp1[:, 1, :], start=True, stop=True)\
                                .then_inc(full("B", f"{kind}{l}{m}"), 1)
                    yield at_l + UNITS_END + 4
                    if used("B", f"fd{l}", i):
                        pe.wait_ge(*vacant("B", f"fd{l}", i))
                    b = bank("B", f"fd{l}")
                    for m, (at, n) in enumerate(HT):
                        pe.wait_ge(*step("f_ha", i, 3 * l + m + 1))
                        last = mm(b[:, :], w(f"w2_{l}", m * D, m * D + D, rows=slice(0, n)), sqk[0:n, 0, m, :],
                                  start=(m == 0), stop=(m == 2))
                    last.then_inc(full("B", f"fd{l}"), 1)
                yield B_END + 1
                pe.wait_ge(*step("x2", i))
                if used("B", "xo", i):
                    pe.wait_ge(*vacant("B", "xo", i))
                b = bank("B", "xo")
                for q in range(NT):
                    last = nc.tensor.transpose(b[:, q * P:(q + 1) * P], x2[:, q * P:(q + 1) * P], ident)
                last.then_inc(full("B", "xo"), 1)

            run(pe, stage_a, stage_b)

        @block.scalar
        def _(act):
            f = nc.scalar.activation
            act.wait_ge(sem("weights"), 16)
            act.wait_ge(sem("rows"), 16)

            def shifted(dst, src, name, after, i, k):
                act.wait_ge(*step(after, i, k))
                nc.scalar.copy(dst[0:64, 0:T], src[0:64, :]).then_inc(sem(name), 1)
                nc.scalar.copy(dst[64:P, 1:T + 1], src[64:P, :]).then_inc(sem(name), 1)

            f(neg_a[:, :], w("alog"), ACT.Exp).then_inc(sem("expA"), 1)
            f(neg_am[:, :], alog_row, ACT.Exp).then_inc(sem("expA"), 1)
            act.wait_ge(sem("setup"), SETUP)

            def stage_a(i):
                act.wait_ge(*filled("A", "xT", i))
                b = bank("A", "xT")
                if later(i):
                    act.wait_ge(*before("a_x1", i))
                nc.scalar.copy(xT[:, :], b[:, :]).then_inc(sem("a_xT"), 1)
                yield 1
                act.wait_ge(*step("a_xc", i))
                f(xsq[:, :], xc[:, :], ACT.Square).then_inc(sem("a_xsq"), 1)
                yield 2
                act.wait_ge(*filled("A", "var", i))
                b = bank("A", "var")
                f(xsq[:, :], b[:, :], ACT.Ln, bias=col_eps[:, 0:1]).then_inc(sem("a_ln"), 1)
                act.wait_ge(*step("a_ln", i))
                f(rstd[:, :], xsq[:, :], ACT.Exp, scale=-0.5).then_inc(sem("a_rstd"), 1)
                yield 3
                act.wait_ge(*filled("A", "dlow", i))
                b = bank("A", "dlow")
                nc.scalar.copy(dlow[0:64, :], b[0:64, :]).then_inc(sem("a_dlow"), 1)
                for d in range(2):
                    act.wait_ge(*filled("A", f"bc{d}", i))
                    b = bank("A", f"bc{d}")
                    nc.scalar.copy(parts[0:96, d, :], b[0:96, :]).then_inc(sem("a_bch"), 1)
                yield 4
                for d in range(2):
                    act.wait_ge(*filled("A", f"z{d}", i))
                    b = bank("A", f"z{d}")
                    f(ez[:, d, :], b[:, :], ACT.Abs, bias=w("dtb", d, d + 1)).then_inc(sem("a_zabs"), 1)
                    f(zrel[:, d, :], b[:, :], ACT.Relu, bias=w("dtb", d, d + 1)).then_inc(sem("a_zrel"), 1)
                yield 5
                act.wait_ge(*step("a_zabs", i))
                f(ez[:, :, :], ez[:, :, :], ACT.Exp, scale=-1.0).then_inc(sem("a_ez"), 1)
                act.wait_ge(*step("a_ez", i))
                f(delta[:, :, :], ez[:, :, :], ACT.Ln, bias=col_one[:, 0:1]).then_inc(sem("a_lz"), 1)
                act.wait_ge(*step("a_rd", i))
                f(rt[:, 1], rt[:, 0], ACT.Exp).then_inc(sem("a_re"), 1)
                for m in range(4):
                    yield 5 + m // 2
                    act.wait_ge(*filled("A", f"up{m}", i))
                    b = bank("A", f"up{m}")
                    if m >= 2:
                        act.wait_ge(*step("a_down", i, m - 1))
                    f(h1[:, m % 2, :], b[:, :], ACT.Gelu_apprx_tanh, bias=w("b1", m, m + 1)).then_inc(sem("a_h1"), 1)
                yield 7
                act.wait_ge(*filled("A", "rbc", i))
                b = bank("A", "rbc")
                nc.scalar.copy(rbc[:, :], b[:, :]).then_inc(sem("a_rbc"), 1)
                yield 8
                act.wait_ge(*step("a_fo", i))
                f(gate[:, :], fo[:, :], ACT.Silu).then_inc(sem("a_gate"), 1)
                yield SCAN
                act.wait_ge(*step("a_delta", i))
                for k in range(2 * NS):
                    yield SCAN + k
                    if k >= 2:
                        act.wait_ge(*step("a_h", i, k - 1))
                    f(dA[:, k % 2, :], delta[:, k // NS, :], ACT.Exp, scale=neg_a[:, k:k + 1])\
                        .then_inc(sem("a_dA"), 1)
                    act.wait_ge(*filled("A", f"C{k}", i))
                    b = bank("A", f"C{k}")
                    if k >= 2:
                        act.wait_ge(*step("a_hc", i, k - 1))
                    nc.scalar.copy(Cs[:, k % 2, :], b[:, :]).then_inc(sem("a_Cs"), 1)

            def stage_b(i):
                act.wait_ge(*step("a_x1", i))
                if later(i):
                    act.wait_ge(*before("x2", i))
                nc.scalar.copy(x1b[:, :], x1[:, :]).then_inc(sem("m_x1b"), 1)
                act.wait_ge(*step("m_xc", i))
                f(tmp2[:, 0, :], tmp1[:, 0, :], ACT.Square).then_inc(sem("m_xsq"), 1)
                yield 1
                act.wait_ge(*filled("B", "var", i))
                b = bank("B", "var")
                f(rsB[:, :], b[:, :], ACT.Ln, bias=col_eps[:, 0:1]).then_inc(sem("m_ln"), 1)
                act.wait_ge(*step("m_ln", i))
                f(rsB[:, :], rsB[:, :], ACT.Exp, scale=-0.5).then_inc(sem("m_r"), 1)
                yield 2
                shifted(xs0, xn2, "t_xs", "m_xn", i, 1)
                act.wait_ge(*step("m_q", i))
                f(tmp2[:, 0, :], mq[:, :], ACT.Square).then_inc(sem("m_qsq"), 1)
                yield 3
                act.wait_ge(*filled("B", "mss", i))
                b = bank("B", "mss")
                f(rsB[:, :], b[:, :], ACT.Ln, bias=col_eps[:, 0:1]).then_inc(sem("m_qln"), 1)
                act.wait_ge(*step("m_qln", i))
                f(rsB[:, :], rsB[:, :], ACT.Exp, scale=-0.5).then_inc(sem("m_qr"), 1)
                for t in range(4):
                    yield 4 + t // 2
                    act.wait_ge(*filled("B", f"cx{t}", i))
                    b = bank("B", f"cx{t}")
                    f(xbc[:, t, :], b[:, :], ACT.Silu, bias=w("convb", t, t + 1)).then_inc(sem("m_xs"), 1)
                for t in range(2):
                    act.wait_ge(*filled("B", f"mz{t}", i))
                    b = bank("B", f"mz{t}")
                    f(sz[:, t, :], b[:, :], ACT.Silu).then_inc(sem("m_sz"), 1)
                yield 7
                act.wait_ge(*step("m_dtz", i))
                f(dtk[:, 1], dtk[:, 0], ACT.Abs).then_inc(sem("m_dabs"), 1)
                act.wait_ge(*step("m_dabs", i))
                f(dtk[:, 2], dtk[:, 1], ACT.Exp, scale=-1.0).then_inc(sem("m_dez"), 1)
                act.wait_ge(*step("m_dez", i))
                f(dtk[:, 3], dtk[:, 2], ACT.Ln, bias=col_one[:, 0:1]).then_inc(sem("m_dln"), 1)
                yield 9
                act.wait_ge(*filled("B", "acl", i))
                b = bank("B", "acl")
                f(etot[:, :], b[:, 0:16], ACT.Exp).then_inc(sem("m_etot"), 1)
                act.wait_ge(*step("m_dlast", i))
                f(decay[:, :], dlast[:, :], ACT.Exp).then_inc(sem("m_decay"), 1)
                for q in range(NT):
                    yield 10 + q // 2
                    act.wait_ge(*step("m_ld", i, q + 1))
                    f(big2[:, q], big2[:, q], ACT.Exp).then_inc(sem("m_L"), 1)
                    if q > 0:
                        act.wait_ge(*filled("B", f"ab{q}", i))
                        b = bank("B", f"ab{q}")
                        f(big1[:, q], b[:, :].rearrange("p (h l) -> p h l", h=HM), ACT.Exp).then_inc(sem("m_ea"), 1)
                yield 12
                act.wait_ge(*filled("B", "bt", i))
                b = bank("B", "bt")
                nc.scalar.copy(btok[:, :, :], b[:, :].rearrange("p (q n) -> p q n", q=NT)).then_inc(sem("m_bt"), 1)
                yield 14
                for g in range(2):
                    act.wait_ge(*step("m_y3", i, g + 1))
                    f(tmp2[:, g, :], y3[:, g, :], ACT.Square).then_inc(sem("m_ysq"), 1)
                yield 15
                act.wait_ge(*filled("B", "yss", i))
                b = bank("B", "yss")
                f(rsB[:, :], b[:, :], ACT.Ln, bias=col_eps[:, 0:1]).then_inc(sem("m_yln"), 1)
                act.wait_ge(*step("m_yln", i))
                f(rsB[:, :], rsB[:, :], ACT.Exp, scale=-0.5).then_inc(sem("m_yr"), 1)
                for l in range(NL):
                    at_l = LAYER + l * LAYER_SLOTS
                    for m in range(4):
                        yield at_l + m
                        for kind, (job, done) in enumerate((("q", "t_qsq"), ("k", "t_ksq"))):
                            act.wait_ge(*filled("B", f"{job}{l}{m}", i))
                            b = bank("B", f"{job}{l}{m}")
                            f(sqk[:, kind, m, :], b[:, :], ACT.Square).then_inc(sem(done), 1)
                    yield at_l + 4
                    act.wait_ge(*filled("B", f"nrm{l}", i))
                    b = bank("B", f"nrm{l}")
                    f(nrm[:, 0, :], b[:, 0:64], ACT.Sqrt).then_inc(sem("t_nrm"), 1)
                    for q in range(NT):
                        yield at_l + 4 + q // 2
                        act.wait_ge(*filled("B", f"v{l}{q}", i))
                        b = bank("B", f"v{l}{q}")
                        nc.scalar.copy(vt[:, q, :], b[:, :]).then_inc(sem("t_v"), 1)
                    for q in range(1, NT):
                        yield at_l + 5 + q // 2
                        act.wait_ge(*filled("B", f"vh{l}{q}", i))
                        b = bank("B", f"vh{l}{q}")
                        nc.scalar.copy(vbd[0:WIN, q - 1, :, 0:DH],
                                       b[0:WIN, 0:256].rearrange("p (g d) -> p g d", g=4)).then_inc(sem("t_vh"), 1)
                        odd = vt[WIN:P, q - 1, :].rearrange("p (g two d) -> p g two d", two=2, d=DH)[:, :, 1, :]
                        act.wait_ge(*step("t_v", i, 4 * l + q))
                        nc.scalar.copy(vbd[WIN:P, q - 1, :, DH:P], odd).then_inc(sem("t_vo"), 1)
                    for n in range(NU + LAG_V + 1):
                        yield at_l + UNIT + n
                        if n < NU:
                            q, g = UNITS[n]
                            act.wait_ge(*step("t_bias", i, NU * l + n + 1))
                            if g == 0 and q >= 2:
                                act.wait_ge(*step("t_rinv", i, 4 * l + q - 1))
                            b = bank("B", f"S{l}_{n}")
                            wd = P if q == 0 else P + WIN
                            for hh in range(2):
                                at = 8 * q + 2 * g + hh
                                last = f(Pm[:, n % 3, hh * wd:(hh + 1) * wd], b[:, hh * wd:(hh + 1) * wd], ACT.Exp,
                                         bias=bias[:, n % 4, hh:hh + 1], scale=rq8[:, at:at + 1],
                                         accum_out=rsum[:, q % 2, g, hh:hh + 1])
                            last.then_inc(sem("t_P"), 1)
                        if LAG_T <= n < NU + LAG_T:
                            k = n - LAG_T
                            wd = 256 if UNITS[k][0] == 0 else 384
                            act.wait_ge(*filled("B", f"PT{l}_{k}", i))
                            b = bank("B", f"PT{l}_{k}")
                            if k >= 2:
                                act.wait_ge(*step("t_O", i, NU * l + k - 1))
                            nc.scalar.copy(PT[:, k % 2, 0:wd], b[:, 0:wd]).then_inc(sem("t_PT"), 1)
                        if n > LAG_V and (n - LAG_V) % 4 == 0:
                            q = (n - LAG_V) // 4 - 1
                            act.wait_ge(*filled("B", f"oT{l}{q}", i))
                            b = bank("B", f"oT{l}{q}")
                            nc.scalar.copy(oT[:, :, q * P:(q + 1) * P], b[:, :].rearrange("p (m t) -> p m t", m=4))\
                                .then_inc(sem("t_oT"), 1)
                    yield at_l + UNITS_END
                    shifted(xsA, xa, "f_xs", "f_xa", i, l + 1)
                    yield at_l + UNITS_END + 1
                    act.wait_ge(*step("f_xc", i, l + 1))
                    f(tmp2[:, 0, :], tmp1[:, 0, :], ACT.Square).then_inc(sem("f_sq"), 1)
                    yield at_l + UNITS_END + 2
                    act.wait_ge(*filled("B", f"lvar{l}", i))
                    b = bank("B", f"lvar{l}")
                    f(rsB[:, :], b[:, :], ACT.Ln, bias=col_eps[:, 0:1]).then_inc(sem("f_ln"), 1)
                    act.wait_ge(*step("f_ln", i, l + 1))
                    f(rsB[:, :], rsB[:, :], ACT.Exp, scale=-0.5).then_inc(sem("f_r"), 1)
                    yield at_l + UNITS_END + 3
                    for m, (at, n) in enumerate(HT):
                        act.wait_ge(*filled("B", f"fg{l}{m}", i))
                        b = bank("B", f"fg{l}{m}")
                        if m >= 2:
                            act.wait_ge(*step("f_ha", i, 3 * l + m - 1))
                        f(gl[0:n, m % 2, :], b[0:n, :], ACT.Gelu, bias=w(f"fb1_{l}", 3 + m, 4 + m, rows=slice(0, n)))\
                            .then_inc(sem("f_gl"), 1)
                    yield at_l + UNITS_END + 4
                    if l + 1 < NL:
                        shifted(xs0, yB, "t_xs", "f_y", i, l + 1)
                yield B_END
                act.wait_ge(*step("f_y", i, NL))
                f(tmp2[:, 0, :], yB[:, :], ACT.Silu).then_inc(sem("g2"), 1)
                yield B_END + 1
                act.wait_ge(*filled("B", "xo", i))
                b = bank("B", "xo")
                if later(i):
                    act.wait_ge(*before("store", i))
                nc.scalar.copy(xo[:, :], b[:, :]).then_inc(sem("xo"), 1)

            run(act, stage_a, stage_b)

        @block.vector
        def _(dve):
            v = nc.vector
            steps = [0]

            def done(ins):
                steps[0] += 1
                ins.then_inc(sem("setup"), 1)
                dve.wait_ge(sem("setup"), steps[0])

            done(v.memset(inv128[:, :], 1.0 / D))
            done(v.memset(inv256[:, :], 1.0 / DI))
            done(v.memset(col_eps[:, :], EPS))
            done(v.memset(col_one[:, :], 1.0))
            done(v.memset(hpad[:, :], 0.0))
            done(v.memset(xs0[:, :], 0.0))
            done(v.memset(vbd[:, :, :, :], 0.0))
            dve.wait_ge(sem("consts"), 16)
            dve.wait_ge(sem("weights"), 16)
            dve.wait_ge(sem("taps"), 16)
            dve.wait_ge(sem("tables"), 16 * NL)
            dve.wait_ge(sem("expA"), 2)
            done(v.tensor_copy(ident16[:, :], ident))
            dve.wait_ge(sem("mask"), 16)
            done(v.tensor_copy(mask16[:, :], Pm[:, 0, :]))
            done(v.tensor_copy(sel16[0:96, :], c("selbase", rows=slice(0, 96))))
            done(v.tensor_scalar(neg_a[:, :], neg_a[:, :], -1.0, None, ALU.mult))
            done(v.tensor_scalar(neg_am[:, :], neg_am[:, :], -1.0, None, ALU.mult))
            done(v.tensor_tensor(dsum[:, :], w("Dfb", 0, 1), w("Dfb", 1, 2), ALU.add))
            done(v.tensor_scalar(w("mwz"), w("mwz"), w("npre"), None, ALU.mult))
            done(v.tensor_scalar(w("mwc"), w("mwc"), w("npre"), None, ALU.mult))
            for k in range(TAPS):
                done(v.tensor_tensor(wc_f[:, k, :], w("mwc"), wc_f[:, k, :], ALU.mult))
            done(v.tensor_scalar(w("mwdt"), w("mwdt"), w("npre"), None, ALU.mult))
            for g in range(2):
                done(v.tensor_scalar(wout_f[:, g, :], wout_f[:, g, :], w("ngate", g, g + 1), None, ALU.mult))
            for l in range(NL):
                for n in range(len(TABLES)):
                    done(v.tensor_scalar(rot[:, l, n, :], rot[:, l, n, :], w(f"qs{l}", n, n + 1), None, ALU.mult))
            assert steps[0] == SETUP

            def stage_a(i):
                yield 1
                dve.wait_ge(*filled("A", "mean", i))
                b = bank("A", "mean")
                v.tensor_tensor(xc[:, :], xT[:, :], b[:, :], ALU.subtract).then_inc(sem("a_xc"), 1)
                yield 2
                dve.wait_ge(*step("a_rstd", i))
                v.tensor_tensor(xn[:, :], xc[:, :], rstd[:, :], ALU.mult).then_inc(sem("a_xn"), 1)
                yield 3
                for d in range(2):
                    dve.wait_ge(*filled("A", f"bc{d}", i))
                    b = bank("A", f"bc{d}")
                    dve.wait_ge(*step("a_bch", i, d + 1))
                    v.tensor_tensor(bcr[0:96, d, :], b[0:96, :], parts[0:96, d, :], ALU.subtract)\
                        .then_inc(sem("a_bcr"), 1)
                dve.wait_ge(*step("a_bcr", i))
                for r in (slice(32, 64), slice(64, 96)):
                    v.tensor_copy(parts[r, :, :], bcr[r, :, :]).then_inc(sem("a_mid"), 1)
                yield 4
                dve.wait_ge(*filled("A", "router", i))
                b = bank("A", "router")
                lg = b[:, 0:NT * NE].rearrange("p (q e) -> p q e", q=NT)
                v.tensor_reduce(rs[:, 0, :], lg, AX.X, ALU.max).then_inc(sem("a_rmax"), 1)
                dve.wait_ge(*step("a_rmax", i))
                v.tensor_tensor(rt[:, 0], lg, over(rs[:, 0, :], NE), ALU.subtract).then_inc(sem("a_rd"), 1)
                yield 5
                dve.wait_ge(*step("a_re", i))
                v.tensor_reduce(rs[:, 1, :], rt[:, 1], AX.X, ALU.add).then_inc(sem("a_rsum"), 1)
                dve.wait_ge(*step("a_rsum", i))
                v.reciprocal(rs[:, 2, :], rs[:, 1, :]).then_inc(sem("a_rrec"), 1)
                dve.wait_ge(*step("a_rrec", i))
                v.tensor_tensor(rt[:, 2], rt[:, 1], over(rs[:, 2, :], NE), ALU.mult).then_inc(sem("a_rp"), 1)
                wait_alone(dve, "a_rp", i)
                for q in range(NT):
                    v.max(rt[:, 3, q, :], rt[:, 2, q, :]).then_inc(sem("a_top"), 1)
                dve.wait_ge(*step("a_top", i))
                v.tensor_tensor(rs[:, 3, :], rt[:, 3, :, 0], rt[:, 3, :, 1], ALU.add).then_inc(sem("a_r2"), 1)
                dve.wait_ge(*step("a_r2", i))
                v.reciprocal(rs[:, 4, :], rs[:, 3, :]).then_inc(sem("a_r2r"), 1)
                dve.wait_ge(*step("a_r2r", i))
                v.tensor_tensor(rw[:, :, :], rt[:, 3, :, 0:2], over(rs[:, 4, :], 2), ALU.mult).then_inc(sem("a_rw"), 1)
                dve.wait_ge(*step("a_rw", i))
                v.tensor_tensor(rs[:, 5, :], rw[:, :, 0], rw[:, :, 1], ALU.add).then_inc(sem("a_rfac"), 1)
                yield 6
                dve.wait_ge(*step("a_ez", i))
                v.tensor_scalar(zp[:, :, :], ez[:, :, :], 1.0 / 3, -0.5, ALU.mult, ALU.add).then_inc(sem("a_p1"), 1)
                v.tensor_scalar(zmask[:, :, :], ez[:, :, :], 1.0 / 128, None, ALU.is_lt).then_inc(sem("a_zm"), 1)
                dve.wait_ge(*step("a_p1", i))
                v.tensor_tensor(zp[:, :, :], zp[:, :, :], ez[:, :, :], ALU.mult).then_inc(sem("a_p2"), 1)
                dve.wait_ge(*step("a_p2", i))
                v.scalar_tensor_tensor(out=zp[:, :, :], in0=zp[:, :, :], scalar=1.0, in1=ez[:, :, :],
                                       op0=ALU.add, op1=ALU.mult).then_inc(sem("a_p3"), 1)
                wait_alone(dve, "a_p3", i)
                dve.wait_ge(*step("a_zm", i))
                dve.wait_ge(*step("a_lz", i))
                v.copy_predicated(delta[:, :, :], zmask[:, :, :], zp[:, :, :]).then_inc(sem("a_lsel"), 1)
                dve.wait_ge(*step("a_lsel", i))
                dve.wait_ge(*step("a_zrel", i))
                v.tensor_tensor(delta[:, :, :], delta[:, :, :], zrel[:, :, :], ALU.add).then_inc(sem("a_delta"), 1)
                dve.wait_ge(*step("a_delta", i))
                v.tensor_tensor(u[:, :, :], delta[:, :, :], each(xn[:, :], 2), ALU.mult).then_inc(sem("a_u"), 1)
                yield 7
                dve.wait_ge(*step("a_down", i))
                dve.wait_ge(*step("a_rbc", i))
                v.scalar_tensor_tensor(out=fo[:, :], in0=y_acc[:, :], scalar=w("b2"), in1=rbc[:, :],
                                       op0=ALU.add, op1=ALU.mult).then_inc(sem("a_fo"), 1)
                yield SCAN
                dve.wait_ge(*step("a_u", i))
                for k in range(2 * NS):
                    yield SCAN + k
                    d = k // NS
                    dve.wait_ge(*filled("A", f"B{k}", i))
                    b = bank("A", f"B{k}")
                    v.tensor_tensor(bx[:, k % 2, :], u[:, d, :], b[:, :], ALU.mult).then_inc(sem("a_bx"), 1)
                    dve.wait_ge(*step("a_bx", i, k + 1))
                    dve.wait_ge(*step("a_dA", i, k + 1))
                    if k >= 2:
                        dve.wait_ge(*step("a_hc", i, k - 1))
                    o, a, b = hst[:, k % 2, :], dA[:, k % 2, :], bx[:, k % 2, :]
                    if d:
                        o, a, b = o[:, ::-1], a[:, ::-1], b[:, ::-1]
                    v.tensor_tensor_scan(o, a, b, 0.0, ALU.mult, ALU.add).then_inc(sem("a_h"), 1)
                yield A_END
                dve.wait_ge(*step("a_yacc", i))
                v.scalar_tensor_tensor(out=ys[:, :], in0=xn[:, :], scalar=dsum[:, 0:1], in1=y_acc[:, :],
                                       op0=ALU.mult, op1=ALU.add).then_inc(sem("a_y"), 1)
                dve.wait_ge(*step("a_y", i))
                dve.wait_ge(*step("a_gate", i))
                v.tensor_tensor(ys[:, :], ys[:, :], gate[:, :], ALU.mult).then_inc(sem("a_yg"), 1)
                dve.wait_ge(*step("a_yg", i))
                if later(i):
                    dve.wait_ge(*before("m_x1b", i))
                v.tensor_tensor(x1[:, :], xT[:, :], ys[:, :], ALU.add).then_inc(sem("a_x1"), 1)

            def stage_b(i):
                dve.wait_ge(*filled("B", "mean", i))
                b = bank("B", "mean")
                v.tensor_tensor(tmp1[:, 0, :], x1b[:, :], b[:, :], ALU.subtract).then_inc(sem("m_xc"), 1)
                yield 1
                dve.wait_ge(*step("m_r", i))
                v.tensor_tensor(xn2[:, :], tmp1[:, 0, :], rsB[:, :], ALU.mult).then_inc(sem("m_xn"), 1)
                yield 2
                dve.wait_ge(*filled("B", "mq", i))
                b = bank("B", "mq")
                v.tensor_tensor(tmp1[:, 1, :], b[:, :], c("mcos"), ALU.mult).then_inc(sem("m_t1"), 1)
                dve.wait_ge(*filled("B", "mqr", i))
                b = bank("B", "mqr")
                v.tensor_tensor(tmp2[:, 1, :], b[:, :], c("msin"), ALU.mult).then_inc(sem("m_t2"), 1)
                yield 3
                dve.wait_ge(*step("m_qr", i))
                v.tensor_tensor(hpad[:, 3:3 + T], mq[:, :], rsB[:, :], ALU.mult).then_inc(sem("m_h"), 1)
                yield 6
                dve.wait_ge(*filled("B", "mdt", i))
                b = bank("B", "mdt")
                v.tensor_tensor(dtk[:, 0], b[:, 0:16], dtb_row, ALU.add).then_inc(sem("m_dtz"), 1)
                dve.wait_ge(*step("m_dtz", i))
                v.tensor_scalar(dtk[:, 4], dtk[:, 0], 0.0, None, ALU.max).then_inc(sem("m_drel"), 1)
                yield 7
                dve.wait_ge(*step("m_dez", i))
                v.tensor_scalar(dtk[:, 5], dtk[:, 2], 1.0 / 3, -0.5, ALU.mult, ALU.add).then_inc(sem("m_dp1"), 1)
                v.tensor_scalar(dtm[:, :], dtk[:, 2], 1.0 / 128, None, ALU.is_lt).then_inc(sem("m_dm"), 1)
                dve.wait_ge(*step("m_dp1", i))
                v.tensor_tensor(dtk[:, 6], dtk[:, 5], dtk[:, 2], ALU.mult).then_inc(sem("m_dp2"), 1)
                dve.wait_ge(*step("m_dp2", i))
                v.scalar_tensor_tensor(out=dtk[:, 7], in0=dtk[:, 6], scalar=1.0, in1=dtk[:, 2],
                                       op0=ALU.add, op1=ALU.mult).then_inc(sem("m_dp3"), 1)
                wait_alone(dve, "m_dp3", i)
                dve.wait_ge(*step("m_dm", i))
                dve.wait_ge(*step("m_dln", i))
                v.copy_predicated(dtk[:, 3], dtm[:, :], dtk[:, 7]).then_inc(sem("m_dsel"), 1)
                dve.wait_ge(*step("m_dsel", i))
                dve.wait_ge(*step("m_drel", i))
                v.tensor_tensor(dt[:, :], dtk[:, 3], dtk[:, 4], ALU.add).then_inc(sem("m_dt"), 1)
                dve.wait_ge(*step("m_dt", i))
                v.tensor_tensor(dta[:, :], dt[:, :], neg_am[:, :], ALU.mult).then_inc(sem("m_dta"), 1)
                yield 8
                dve.wait_ge(*filled("B", "acs", i))
                b = bank("B", "acs")
                v.tensor_copy(acs[:, :], b[:, 0:16]).then_inc(sem("m_acs"), 1)
                yield 9
                dve.wait_ge(*filled("B", "acl", i))
                b = bank("B", "acl")
                dve.wait_ge(*step("m_etot", i))
                dve.wait_ge(*step("m_acs", i))
                v.tensor_tensor(dlast[:, :], b[:, 0:16], acs[:, :], ALU.subtract).then_inc(sem("m_dlast"), 1)
                for q in range(NT):
                    yield 9 + q // 2
                    dve.wait_ge(*filled("B", f"ab{q}", i))
                    b = bank("B", f"ab{q}")
                    for h in range(HM):
                        n = q * HM + h
                        last = v.tensor_scalar(big2[:, q, h, :], b[:, h * P:(h + 1) * P], acs[:, n:n + 1], 0.0,
                                               ALU.subtract, ALU.min)
                    last.then_inc(sem("m_ld"), 1)
                yield 11
                dve.wait_ge(*filled("B", "G", i))
                b = bank("B", "G")
                v.tensor_tensor(Gm[:, :, :], b[:, :].rearrange("p (q l) -> p q l", q=NT), each(c("tri"), NT),
                                ALU.mult).then_inc(sem("m_G"), 1)
                yield 12
                for g in range(2):
                    dve.wait_ge(*filled("B", f"xt{g}", i))
                    b = bank("B", f"xt{g}")
                    dts = dt[:, :].rearrange("p (q h) -> p q h", q=NT)[:, :, 2 * g:2 * g + 2]
                    v.tensor_tensor(xdt[:, :, 2 * g:2 * g + 2, :],
                                    b[:, :].rearrange("p (q h d) -> p q h d", q=NT, h=2),
                                    dts.unsqueeze(3).to_broadcast([P, NT, 2, PM]), ALU.mult)\
                        .then_inc(sem("m_xdt"), 1)
                dve.wait_ge(*step("m_G", i))
                for q in range(NT):
                    dve.wait_ge(*step("m_L", i, q + 1))
                    v.tensor_tensor(big2[:, q], big2[:, q], each(Gm[:, q, :], HM), ALU.mult).then_inc(sem("m_M"), 1)
                yield 13
                for q in range(NT - 1):
                    dve.wait_ge(*filled("B", f"st{q}", i))
                    b = bank("B", f"st{q}")
                    add = b[:, 0:256].rearrange("p (h d) -> p h d", h=HM)
                    if q == 0:
                        v.tensor_copy(st[:, 0], add).then_inc(sem("m_st"), 1)
                    else:
                        dve.wait_ge(*step("m_st", i, q))
                        v.tensor_tensor(sttmp[:, :, :], st[:, q - 1], over(etot[:, q * HM:(q + 1) * HM], PM), ALU.mult)\
                            .then_inc(sem("m_sttmp"), 1)
                        dve.wait_ge(*step("m_sttmp", i, q))
                        v.tensor_tensor(st[:, q], sttmp[:, :, :], add, ALU.add).then_inc(sem("m_st"), 1)
                yield 14
                for g in range(2):
                    dve.wait_ge(*filled("B", f"y{g}", i))
                    b = bank("B", f"y{g}")
                    v.scalar_tensor_tensor(out=tmp1[:, g, :], in0=xbc[:, g, :], scalar=w("mD", g, g + 1), in1=b[:, :],
                                           op0=ALU.mult, op1=ALU.add).then_inc(sem("m_y2"), 1)
                yield 15
                dve.wait_ge(*filled("B", "mo", i))
                b = bank("B", "mo")
                dve.wait_ge(*step("m_yr", i))
                v.tensor_tensor(tmp1[:, 0, :], b[:, :], rsB[:, :], ALU.mult).then_inc(sem("m_sm1"), 1)
                for l in range(NL):
                    xin = xn2 if l == 0 else yB
                    at_l = LAYER + l * LAYER_SLOTS
                    yield at_l
                    if l == 0:
                        dve.wait_ge(*step("m_sm", i))
                    for m in range(4):
                        yield at_l + m
                        for kind, (job, sq, dc, dr, summed) in enumerate((("q", "t_qsq", "t_qc", "t_qr", "t_q"),
                                                                          ("k", "t_ksq", "t_kc", "t_kr", "t_ksum"))):
                            s = kind
                            dve.wait_ge(*filled("B", f"{job}{l}{m}", i))
                            b = bank("B", f"{job}{l}{m}")
                            dve.wait_ge(*step(sq, i, 4 * l + m + 1))
                            if m >= 1:
                                dve.wait_ge(*step(summed, i, 4 * l + m))
                            v.tensor_tensor(tmp1[:, s, :], b[:, :], rot[:, l, 2 * kind, :], ALU.mult)\
                                .then_inc(sem(dc), 1)
                            dve.wait_ge(*filled("B", f"{job}r{l}{m}", i))
                            b = bank("B", f"{job}r{l}{m}")
                            v.tensor_tensor(tmp2[:, s, :], b[:, :], rot[:, l, 2 * kind + 1, :], ALU.mult)\
                                .then_inc(sem(dr), 1)
                    yield at_l + 4
                    dve.wait_ge(*step("t_nrm", i, l + 1))
                    v.tensor_scalar(nrm[:, 1, :], nrm[:, 0, :], 1e-12, None, ALU.max).then_inc(sem("t_clip"), 1)
                    dve.wait_ge(*step("t_clip", i, l + 1))
                    v.reciprocal(nrm[:, 2, :], nrm[:, 1, :]).then_inc(sem("t_rqk"), 1)
                    dve.wait_ge(*step("t_rqk", i, l + 1))
                    v.tensor_scalar(rq8[:, :], nrm[:, 2, 0:32], 8.0, None, ALU.mult).then_inc(sem("t_rq8"), 1)
                    for m in range(4):
                        yield at_l + 6 + m // 2
                        dve.wait_ge(*filled("B", f"rk{l}{m}", i))
                        b = bank("B", f"rk{l}{m}")
                        dve.wait_ge(*step("t_ksum", i, 4 * l + m + 1))
                        v.tensor_tensor(qk[:, 1, m, :], qk[:, 1, m, :], b[:, :], ALU.mult).then_inc(sem("t_k"), 1)
                    dve.wait_ge(*step("t_rq8", i, l + 1))
                    for n in range(NU + LAG_V + 1):
                        yield at_l + UNIT + n
                        if n < NU:
                            q, g = UNITS[n]
                            dve.wait_ge(*filled("B", f"S{l}_{n}", i))
                            b = bank("B", f"S{l}_{n}")
                            wd = P if q == 0 else P + WIN
                            v.tensor_reduce(mx[:, n % 4, :], b[:, 0:2 * wd].rearrange("p (h j) -> p h j", h=2),
                                            AX.X, ALU.max).then_inc(sem("t_max"), 1)
                            dve.wait_ge(*step("t_max", i, NU * l + n + 1))
                            at = 8 * q + 2 * g
                            v.scalar_tensor_tensor(out=bias[:, n % 4, :], in0=mx[:, n % 4, :], scalar=-1.0,
                                                   in1=rq8[:, at:at + 2], op0=ALU.mult, op1=ALU.mult)\
                                .then_inc(sem("t_bias"), 1)
                        if n >= LAG_V and (n - LAG_V) % 4 == 3 and n < NU + LAG_V:
                            q = (n - LAG_V) // 4
                            dve.wait_ge(*step("t_P", i, NU * l + 4 * q + 4))
                            v.reciprocal(rinv[:, q % 2, :], rsum[:, q % 2].rearrange("p g h -> p (g h)"))\
                                .then_inc(sem("t_rinv"), 1)
                            dve.wait_ge(*step("t_rinv", i, 4 * l + q + 1))
                            dve.wait_ge(*step("t_O", i, NU * l + 4 * q + 4))
                            if q >= 2:
                                dve.wait_ge(*step("t_oT", i, 4 * l + q - 1))
                            v.tensor_tensor(on[:, q % 2, :].rearrange("p (h d) -> p h d", h=HA),
                                            o_acc[:, :].rearrange("p (h d) -> p h d", h=HA),
                                            over(rinv[:, q % 2, :], DH), ALU.mult).then_inc(sem("t_on"), 1)
                    yield at_l + UNITS_END
                    dve.wait_ge(*filled("B", f"wo{l}", i))
                    b = bank("B", f"wo{l}")
                    if l == 0:
                        if later(i):
                            dve.wait_ge(*before("store", i))
                    v.tensor_tensor(xa[:, :], xin[:, :], b[:, :], ALU.add).then_inc(sem("f_xa"), 1)
                    yield at_l + UNITS_END + 1
                    dve.wait_ge(*filled("B", f"lmean{l}", i))
                    b = bank("B", f"lmean{l}")
                    v.tensor_tensor(tmp1[:, 0, :], xsA[:, 0:T], b[:, :], ALU.subtract).then_inc(sem("f_xc"), 1)
                    yield at_l + UNITS_END + 2
                    dve.wait_ge(*step("f_r", i, l + 1))
                    v.tensor_tensor(tmp2[:, 1, :], tmp1[:, 0, :], rsB[:, :], ALU.mult).then_inc(sem("f_xr"), 1)
                    dve.wait_ge(*step("f_xr", i, l + 1))
                    v.tensor_scalar(tmp1[:, 1, :], tmp2[:, 1, :], w(f"lg{l}"), w(f"lb{l}"), ALU.mult, ALU.add)\
                        .then_inc(sem("f_hn"), 1)
                    yield at_l + UNITS_END + 3
                    for m, (at, n) in enumerate(HT):
                        dve.wait_ge(*filled("B", f"fa{l}{m}", i))
                        b = bank("B", f"fa{l}{m}")
                        dve.wait_ge(*step("f_gl", i, 3 * l + m + 1))
                        v.scalar_tensor_tensor(out=sqk[0:n, 0, m, :], in0=b[0:n, :],
                                               scalar=w(f"fb1_{l}", m, m + 1, rows=slice(0, n)), in1=gl[0:n, m % 2, :],
                                               op0=ALU.add, op1=ALU.mult).then_inc(sem("f_ha"), 1)
                    yield at_l + UNITS_END + 4
                    dve.wait_ge(*filled("B", f"fd{l}", i))
                    b = bank("B", f"fd{l}")
                    v.scalar_tensor_tensor(out=yB[:, :], in0=b[:, :], scalar=w(f"fb2_{l}"), in1=xa[:, :],
                                           op0=ALU.add, op1=ALU.add).then_inc(sem("f_y"), 1)
                yield B_END
                dve.wait_ge(*step("g2", i))
                v.tensor_tensor(tmp1[:, 0, :], sm[:, :], tmp2[:, 0, :], ALU.mult).then_inc(sem("x2a"), 1)
                dve.wait_ge(*step("x2a", i))
                v.tensor_tensor(x2[:, :], x1b[:, :], tmp1[:, 0, :], ALU.add).then_inc(sem("x2"), 1)

            run(dve, stage_a, stage_b)

        @block.gpsimd
        def _(pool):
            g_ = nc.gpsimd
            pool.wait_ge(sem("setup"), SETUP)
            prior = []

            def stage_a(i):
                yield 4
                pool.wait_ge(*step("a_mid", i))
                if prior:
                    pool.wait_ge(*prior[-1])
                g_.tensor_tensor(parts[64:96, :, :], bcr[64:96, :, :], parts[64:96, :, :], ALU.subtract)\
                    .then_inc(sem("a_parts"), 1)
                prior.append(step("a_parts", i))
                for k in range(2 * NS):
                    yield SCAN + k
                    pool.wait_ge(*step("a_h", i, k + 1))
                    pool.wait_ge(*step("a_Cs", i, k + 1))
                    if k >= 2:
                        pool.wait_ge(*step("a_yacc", i, k - 1))
                    if prior:
                        pool.wait_ge(*prior[-1])
                    g_.tensor_tensor(hc[:, k % 2, :], hst[:, k % 2, :], Cs[:, k % 2, :], ALU.mult)\
                        .then_inc(sem("a_hc"), 1)
                    prior.append(step("a_hc", i, k + 1))

            def stage_b(i):
                prior.clear()
                yield 2
                pool.wait_ge(*step("m_t1", i))
                pool.wait_ge(*step("m_t2", i))
                if prior:
                    pool.wait_ge(*prior[-1])
                g_.tensor_tensor(mq[:, :], tmp1[:, 1, :], tmp2[:, 1, :], ALU.add).then_inc(sem("m_q"), 1)
                prior.append(step("m_q", i))
                yield 11
                for q in range(1, NT):
                    pool.wait_ge(*step("m_ea", i, q))
                    if prior:
                        pool.wait_ge(*prior[-1])
                    g_.tensor_tensor(big1[:, q], big1[:, q], each(xbc[:, 3, q * P:(q + 1) * P], HM), ALU.mult)\
                        .then_inc(sem("m_Ce"), 1)
                    prior.append(step("m_Ce", i, q))
                yield 12
                pool.wait_ge(*step("m_xdt", i))
                pool.wait_ge(*step("m_decay", i))
                if prior:
                    pool.wait_ge(*prior[-1])
                g_.tensor_tensor(xdd[:, :, :, :].rearrange("p q h d -> p (q h) d"),
                                 xdt[:, :, :, :].rearrange("p q h d -> p (q h) d"), over(decay[:, :], PM), ALU.mult)\
                    .then_inc(sem("m_xdd"), 1)
                prior.append(step("m_xdd", i))
                yield 14
                for g in range(2):
                    pool.wait_ge(*step("m_y2", i, g + 1))
                    pool.wait_ge(*step("m_sz", i, g + 1))
                    if prior:
                        pool.wait_ge(*prior[-1])
                    g_.tensor_tensor(y3[:, g, :], tmp1[:, g, :], sz[:, g, :], ALU.mult).then_inc(sem("m_y3"), 1)
                    prior.append(step("m_y3", i, g + 1))
                yield 15
                pool.wait_ge(*step("m_sm1", i))
                if prior:
                    pool.wait_ge(*prior[-1])
                g_.tensor_tensor(sm[:, :], tmp1[:, 0, :], mq[:, :], ALU.add).then_inc(sem("m_sm"), 1)
                prior.append(step("m_sm", i))
                for l in range(NL):
                    for m in range(4):
                        yield LAYER + l * LAYER_SLOTS + m
                        for kind, (dr, summed) in enumerate((("t_qr", "t_q"), ("t_kr", "t_ksum"))):
                            s = kind
                            pool.wait_ge(*step(dr, i, 4 * l + m + 1))
                            if prior:
                                pool.wait_ge(*prior[-1])
                            g_.tensor_tensor(qk[:, kind, m, :], tmp1[:, s, :], tmp2[:, s, :], ALU.add)\
                                .then_inc(sem(summed), 1)
                            prior.append(step(summed, i, 4 * l + m + 1))

            run(pool, stage_a, stage_b)


SETUP = 7 + 3 + 3 + 2 + TAPS + 1 + 2 + len(TABLES) * NL


def shape_constants():
    cp = np.zeros((P, CCOLS), np.float32)

    def put(name, a):
        at, n = COFF[name]
        cp[:a.shape[0], at:at + n] = a

    r = np.arange(P)
    put("ident", np.eye(P, dtype=np.float32))
    put("tri", (r[:, None] <= r[None, :]).astype(np.float32))
    last = np.zeros((P, P), np.float32)
    last[P - 1] = 1.0
    put("lastrow", last)
    put("headsum", (r[:, None] // DH == np.arange(2)[None, :]).astype(np.float32))
    put("selbase", (np.arange(96)[:, None] % 32 == np.arange(32)[None, :]).astype(np.float32))
    j = np.arange(P + WIN)[None, :]
    m = np.where((j >= r[:, None]) & (j <= r[:, None] + WIN), 0.0, MASKED).astype(np.float32)
    mask = np.concatenate([m[:, WIN:], m[:, :WIN], m[:, :WIN], m[:, WIN:]], 1)
    t = np.arange(T, dtype=np.float32)
    inv = np.float32(1.0) / np.float32(10000.0) ** (np.arange(0, 8, 2, dtype=np.float32) / np.float32(8))
    fr = (t[None, :] * inv[:, None]).astype(np.float32)
    put("mcos", np.tile(np.concatenate([np.cos(fr), np.cos(fr)], 0), (16, 1)))
    put("msin", np.tile(np.concatenate([-np.sin(fr), np.sin(fr)], 0), (16, 1)))
    half = np.arange(0, DH, 2, dtype=np.float32)
    inv = np.float32(1.0) / np.float32(10000.0) ** (half / np.float32(DH))
    fr = (t[None, :] * inv[:, None]).astype(np.float32)
    base = (half + np.float32(0.4 * DH)) / np.float32(1.4 * DH)
    sc = (base[:, None] ** ((t - T // 2) / np.float32(WIN // 2))[None, :]).astype(np.float32)
    cos, sin = np.cos(fr), np.sin(fr)
    tables = np.zeros((len(TABLES), P, T), np.float32)
    for name, a in (("cosq", np.concatenate([cos * sc, cos * sc], 0)),
                    ("sinq", np.concatenate([-sin * sc, sin * sc], 0)),
                    ("cosk", np.concatenate([cos / sc, cos / sc], 0)),
                    ("sink", np.concatenate([-sin / sc, sin / sc], 0))):
        tables[TABLES.index(name)] = np.tile(a.astype(np.float32), (2, 1))
    return cp, mask, tables


def lay_out(g):
    wp = np.zeros((P, WCOLS), np.float32)

    def put(name, a):
        at, n = WOFF[name]
        wp[:a.shape[0], at:at + n] = a.reshape(a.shape[0], -1)

    xw, xwb = g["L0_attn_x_proj_w"], g["L0_attn_x_proj_b_w"]
    put("wdelta", np.concatenate([xw[:RK].T, xwb[:RK].T], 1))
    put("wbc", np.concatenate([xw[RK:].T] * 3 + [xwb[RK:].T] * 3, 1))
    put("dtw", np.concatenate([g["L0_attn_dt_proj_w"].T, g["L0_attn_dt_proj_b_w"].T], 0))
    put("dtb", np.stack([g["L0_attn_dt_proj_b"], g["L0_attn_dt_proj_b_b"]], 1))
    put("Dfb", np.stack([g["L0_attn_D"], g["L0_attn_D_b"]], 1))
    put("b1", g["L0_ffn_b1"].reshape(4, P).T)
    put("b2", g["L0_ffn_b2"].reshape(D, 1))
    put("alog", np.concatenate([g["L0_attn_A_log"], g["L0_attn_A_b_log"]], 1))
    put("router", g["L0_ffn_router_w"])
    put("w1", g["L0_ffn_w1"])
    put("w2", g["L0_ffn_w2"].reshape(4, P, D).transpose(1, 0, 2))
    swap8 = np.arange(D) // 8 * 8 + (np.arange(D) + 4) % 8
    wq = g["L1_attn_W_in"][:D]
    put("mwq", wq.T)
    put("mwqr", wq[swap8].T)
    wz = g["L1_attn_W_zxbcdt"]
    put("mwz", wz[:DI].T)
    put("mwc", wz[DI:DI + 512].T)
    put("mwdt", wz[DI + 512:].T)
    put("convb", g["L1_attn_conv_b"].reshape(4, P).T)
    put("mD", np.repeat(g["L1_attn_D_param"], PM).reshape(2, P).T)
    put("npre", g["L1_attn_norm_pre_w"].reshape(D, 1))
    put("ngate", g["L1_attn_norm_gated_w"].reshape(2, P).T)
    put("wout", g["L1_attn_W_out"].T.reshape(2, P, D).transpose(1, 0, 2))
    swap64 = np.arange(INNER) // DH * DH + (np.arange(INNER) + DH // 2) % DH
    for l in range(NL):
        wqkv = g["L1_ffn_wqkv"][l]
        q, k, v = wqkv[:, :INNER], wqkv[:, INNER:2 * INNER], wqkv[:, 2 * INNER:]
        put(f"wq{l}", q)
        put(f"wqr{l}", q[:, swap64])
        put(f"wk{l}", k)
        put(f"wkr{l}", k[:, swap64])
        put(f"wv{l}", v)
        put(f"wo{l}", g["L1_ffn_wo"][l].reshape(4, P, D).transpose(1, 0, 2))
        put(f"w1_{l}", g["L1_ffn_w1"][l])
        b1 = g["L1_ffn_b1"][l]
        for m, (at, n) in enumerate(HT):
            o = WOFF[f"w2_{l}"][0] + m * D
            wp[:n, o:o + D] = g["L1_ffn_w2"][l][at:at + n]
            o = WOFF[f"fb1_{l}"][0]
            wp[:n, o + m] = b1[at:at + n]
            wp[:n, o + 3 + m] = b1[HID + at:HID + at + n]
        put(f"fb2_{l}", g["L1_ffn_b2"][l].reshape(D, 1))
        put(f"lg{l}", g["L1_ffn_ln_g"][l].reshape(D, 1))
        put(f"lb{l}", g["L1_ffn_ln_b"][l].reshape(D, 1))
        qs, ks = np.tile(g["L1_ffn_q_scale"][l], 2), np.tile(g["L1_ffn_k_scale"][l], 2)
        sw = swap64[:P]
        put(f"qs{l}", np.stack([qs, qs[sw], ks, ks[sw]], 1))
    rows = np.concatenate([np.tile(g["L1_attn_dt_bias"], NT), np.tile(g["L1_attn_A_log"], NT)])
    return wp, np.ascontiguousarray(g["L1_attn_conv_w"].T), rows


def kernel(**inputs):
    import concourse.bacc as bacc
    from concourse.bass_utils import run_bass_kernel_spmd

    g = {k: np.asarray(v) for k, v in inputs.items()}
    wp, taps, rows = lay_out(g)
    cp, mask, tables = shape_constants()
    arrays = {"x": np.ascontiguousarray(g["L0_attn_x"]), "wpack": wp, "cpack": cp, "mask": mask,
              "tables": tables, "taps": taps, "rowpack": rows}
    nc = bacc.Bacc("TRN2", target_bir_lowering=False, num_devices=1)
    args = [nc.dram_tensor(k, a.shape, F32, kind="ExternalInput").ap() for k, a in arrays.items()]
    out = nc.dram_tensor("out", (NB, T, D), F32, kind="ExternalOutput").ap()
    build(nc, *args, out)
    return run_bass_kernel_spmd(nc, [arrays], core_ids=[0]).results[0]["out"]
```
